# Optimizing a Trainium2 kernel written in Bass

```python
import numpy as np
import jax
import jax.numpy as jnp

def _softmax(x, axis=-1):
    return jax.nn.softmax(x, axis=axis)

def _gelu(x):
    return jax.nn.gelu(x, approximate=True)

def _silu(x):
    return jax.nn.silu(x)

def _sigmoid(x):
    return jax.nn.sigmoid(x)

def _layernorm(x, axis=-1, eps=1e-05):
    m = jnp.mean(x, axis=axis, keepdims=True)
    v = jnp.var(x, axis=axis, keepdims=True)
    return (x - m) / jnp.sqrt(v + eps)

def _scatter_add(tgt, idx, src, axis=0):
    return tgt.at[idx].add(src)

def _segment_sum(src, seg, n):
    return jax.ops.segment_sum(src, seg, n)
kernel_name = 'mk_gnn_resnorm_d1_gnn_r32_455fe7'

def setup_inputs(seed: int=0):
    np.random.seed(seed)
    _w = jnp.asarray

    def _rec_inputs():
        import jax
        import jax.numpy as jnp
        _gk = jax.random.key(seed)
        x = -0.000202 + 1 * jax.random.normal(jax.random.fold_in(_gk, 1), (3125, 128), jnp.float32)
        _s = jax.random.randint(jax.random.fold_in(_gk, 2), (25000,), 0, 3125, jnp.int32)
        _d = jax.random.randint(jax.random.fold_in(_gk, 3), (25000,), 0, 3125, jnp.int32)
        _loop = jnp.arange(3125, dtype=jnp.int32)
        src = jnp.concatenate([_s, _d, _loop])
        dst = jnp.concatenate([_d, _s, _loop])
        _o = jnp.argsort(dst, stable=True)
        src = src[_o]
        dst = dst[_o]
        return (x, src, dst)
    x, src, dst = _rec_inputs()

    def _L0_gnn_setup():
        import jax, jax.numpy as jnp
        import numpy as np
        N = 50000
        E = 12500
        D_IN = 128
        H = 4
        C = 64
        HC = H * C
        H3 = 6
        D_OUT = 128

        def _gat(x, src, dst, W, a_src, a_dst, b, concat):
            n = x.shape[0]
            h_, c_ = a_src.shape
            h = (x @ W).reshape(n, h_, c_)
            e = (h * a_src).sum(-1)[src] + (h * a_dst).sum(-1)[dst]
            e = jnp.where(e > 0, e, 0.2 * e)
            m = jax.ops.segment_max(e, dst, num_segments=n)
            w = jnp.exp(e - m[dst])
            denom = jax.ops.segment_sum(w, dst, num_segments=n)
            alpha = w / (denom[dst] + 1e-16)
            out = jax.ops.segment_sum(h[src] * alpha[:, :, None], dst, num_segments=n)
            out = out.reshape(n, h_ * c_) if concat else out.mean(axis=1)
            return out + b
        key = jax.random.key(seed)
        ks = jax.random.split(key, 22)
        rn = lambda k, shape, s=0.05: jax.random.normal(k, shape, dtype=jnp.float32) * s
        return {'x': rn(ks[0], (N, D_IN), 1.0), 'edge_index': jax.random.randint(ks[1], (2, E), 0, N, dtype=jnp.int32), 'W1': rn(ks[2], (D_IN, HC)), 'as1': rn(ks[3], (H, C)), 'ad1': rn(ks[4], (H, C)), 'b1': jnp.zeros((HC,), jnp.float32), 's1W': rn(ks[5], (D_IN, HC)), 's1b': jnp.zeros((HC,), jnp.float32), 'W2': rn(ks[6], (HC, HC)), 'as2': rn(ks[7], (H, C)), 'ad2': rn(ks[8], (H, C)), 'b2': jnp.zeros((HC,), jnp.float32), 's2W': rn(ks[9], (HC, HC)), 's2b': jnp.zeros((HC,), jnp.float32), 'W3': rn(ks[10], (HC, H3 * D_OUT)), 'as3': rn(ks[11], (H3, D_OUT)), 'ad3': rn(ks[12], (H3, D_OUT)), 'b3': jnp.zeros((D_OUT,), jnp.float32), 's3W': rn(ks[13], (HC, D_OUT)), 's3b': jnp.zeros((D_OUT,), jnp.float32)}
    _L0_gnn_all = _L0_gnn_setup()
    _L0_gnn_in = {k: v for k, v in _L0_gnn_all.items() if k in ('W1', 'as1', 'ad1', 'b1', 's1W', 's1b', 'W2', 'as2', 'ad2', 'b2', 's2W', 's2b', 'W3', 'as3', 'ad3', 'b3', 's3W', 's3b')}
    del _L0_gnn_all
    return {'x': x, 'src': src, 'dst': dst, 'L0_gnn_W1': _L0_gnn_in['W1'], 'L0_gnn_as1': _L0_gnn_in['as1'], 'L0_gnn_ad1': _L0_gnn_in['ad1'], 'L0_gnn_b1': _L0_gnn_in['b1'], 'L0_gnn_s1W': _L0_gnn_in['s1W'], 'L0_gnn_s1b': _L0_gnn_in['s1b'], 'L0_gnn_W2': _L0_gnn_in['W2'], 'L0_gnn_as2': _L0_gnn_in['as2'], 'L0_gnn_ad2': _L0_gnn_in['ad2'], 'L0_gnn_b2': _L0_gnn_in['b2'], 'L0_gnn_s2W': _L0_gnn_in['s2W'], 'L0_gnn_s2b': _L0_gnn_in['s2b'], 'L0_gnn_W3': _L0_gnn_in['W3'], 'L0_gnn_as3': _L0_gnn_in['as3'], 'L0_gnn_ad3': _L0_gnn_in['ad3'], 'L0_gnn_b3': _L0_gnn_in['b3'], 'L0_gnn_s3W': _L0_gnn_in['s3W'], 'L0_gnn_s3b': _L0_gnn_in['s3b']}

def reference(x, src, dst, L0_gnn_W1, L0_gnn_as1, L0_gnn_ad1, L0_gnn_b1, L0_gnn_s1W, L0_gnn_s1b, L0_gnn_W2, L0_gnn_as2, L0_gnn_ad2, L0_gnn_b2, L0_gnn_s2W, L0_gnn_s2b, L0_gnn_W3, L0_gnn_as3, L0_gnn_ad3, L0_gnn_b3, L0_gnn_s3W, L0_gnn_s3b):
    import jax
    import jax.numpy as jnp

    def _L0_gnn_ref(x, edge_index, W1, as1, ad1, b1, s1W, s1b, W2, as2, ad2, b2, s2W, s2b, W3, as3, ad3, b3, s3W, s3b):
        import jax, jax.numpy as jnp
        import numpy as np
        N = 50000
        E = 12500
        D_IN = 128
        H = 4
        C = 64
        HC = H * C
        H3 = 6
        D_OUT = 128

        def _gat(x, src, dst, W, a_src, a_dst, b, concat):
            n = x.shape[0]
            h_, c_ = a_src.shape
            h = (x @ W).reshape(n, h_, c_)
            e = (h * a_src).sum(-1)[src] + (h * a_dst).sum(-1)[dst]
            e = jnp.where(e > 0, e, 0.2 * e)
            m = jax.ops.segment_max(e, dst, num_segments=n)
            w = jnp.exp(e - m[dst])
            denom = jax.ops.segment_sum(w, dst, num_segments=n)
            alpha = w / (denom[dst] + 1e-16)
            out = jax.ops.segment_sum(h[src] * alpha[:, :, None], dst, num_segments=n)
            out = out.reshape(n, h_ * c_) if concat else out.mean(axis=1)
            return out + b
        n = x.shape[0]
        loops = jnp.arange(n, dtype=edge_index.dtype)
        src = jnp.concatenate([edge_index[0], loops])
        dst = jnp.concatenate([edge_index[1], loops])
        h = jax.nn.elu(_gat(x, src, dst, W1, as1, ad1, b1, True) + x @ s1W + s1b)
        h = jax.nn.elu(_gat(h, src, dst, W2, as2, ad2, b2, True) + h @ s2W + s2b)
        h = jax.nn.elu(_gat(h, src, dst, W3, as3, ad3, b3, False) + h @ s3W + s3b)
        return h
    edge_index = jnp.stack([src, dst])
    x = _layernorm(x + _L0_gnn_ref(x, edge_index, L0_gnn_W1, L0_gnn_as1, L0_gnn_ad1, L0_gnn_b1, L0_gnn_s1W, L0_gnn_s1b, L0_gnn_W2, L0_gnn_as2, L0_gnn_ad2, L0_gnn_b2, L0_gnn_s2W, L0_gnn_s2b, L0_gnn_W3, L0_gnn_as3, L0_gnn_ad3, L0_gnn_b3, L0_gnn_s3W, L0_gnn_s3b), axis=-1)
    return x

_drawn_inputs = setup_inputs


def setup_inputs(seed=0):
    import zlib

    import numpy as np

    out = dict(_drawn_inputs(seed))
    spreads = {'L0_gnn_b1': (0.0, 0.1),
     'L0_gnn_s1b': (0.0, 0.1),
     'L0_gnn_b2': (0.0, 0.1),
     'L0_gnn_s2b': (0.0, 0.1),
     'L0_gnn_b3': (0.0, 0.1),
     'L0_gnn_s3b': (0.0, 0.1)}
    factors = {'L0_gnn_as1': 4.781,
     'L0_gnn_ad1': 8.0,
     'L0_gnn_as2': 7.282,
     'L0_gnn_ad2': 22.82,
     'L0_gnn_as3': 8.0,
     'L0_gnn_ad3': 44.526}
    for name, (base, spread) in spreads.items():
        noise = np.random.default_rng([zlib.crc32(name.encode()), seed]).standard_normal(out[name].shape)
        drawn = base * np.exp(spread * noise) if base else spread * noise
        out[name] = jnp.asarray(drawn.astype(out[name].dtype))
    for name, factor in factors.items():
        out[name] = (out[name] * factor).astype(out[name].dtype)
    return out
```

```python
from contextlib import ExitStack

import numpy as np
import concourse.bass as bass
from concourse import mybir

F32 = mybir.dt.float32
I32 = mybir.dt.int32
ALU = mybir.AluOpType
ACT = mybir.ActivationFunctionType
AX = mybir.AxisListType

P = 128
N = 3125
NB = -(-N // P)
NP = NB * P
E = 53125
TILES = 416
TG = 104
NG4 = TILES // TG
W = 32
GT = P // W
BIG = 1.0e30
SLOPE = 0.2
EPS = 1e-5
D_OUT = 128


class Layer:

    def __init__(self, number, D, H, C, CT):
        self.number, self.D, self.H, self.C, self.CT = number, D, H, C, CT
        self.ND = D // P
        self.HC = H * C
        self.OUT = self.HC if number < 2 else C
        self.ROW = D + H
        self.CHUNKS = TILES // CT
        self.GROUPS = CT // GT
        self.HT = H * CT
        self.tile0 = TILES * number
        self.group0 = self.tile0 // GT
        self.QW = self.ND * H * W
        self.Q = self.ND * H


LAYERS = [Layer(0, 128, 4, 64, 16), Layer(1, 256, 4, 64, 16), Layer(2, 256, 6, 128, 8)]
CHUNK0 = [0, LAYERS[0].CHUNKS, LAYERS[0].CHUNKS + LAYERS[1].CHUNKS]


def wide(ap, axis, shape):
    return ap.unsqueeze(axis).broadcast_to(shape)


def build(nc, x, src, dst, params, out):
    ctx = ExitStack()
    with ctx:
        sems = {}

        def sem(name):
            if name not in sems:
                sems[name] = ctx.enter_context(nc.semaphore(name))
            return sems[name]

        def sb(name, shape, dt=F32):
            return ctx.enter_context(nc.sbuf_tensor(name, shape, dt))

        table = [nc.dram_tensor(f"table{l.number}", (NP, l.ROW), F32, kind="Internal").ap() for l in LAYERS]
        dtable = [nc.dram_tensor(f"dtable{l.number}", (NP, l.H), F32, kind="Internal").ap() for l in LAYERS]
        masks_d = nc.dram_tensor("masks_d", (TILES, 257), F32, kind="Internal").ap()
        joins_d = nc.dram_tensor("joins_d", (2, TILES), F32, kind="Internal").ap()

        acc = sb("acc", [P, 12 * NP])
        dm = sb("dm", [12, NP])
        ring = sb("ring", [P, 4224])
        idx = sb("idx", [P, TILES], I32)
        islot = sb("islot", [P, 2, 16], I32)
        dloc = sb("dloc", [P, TILES])
        lastE = sb("lastE", [P, TILES])
        baseI = sb("baseI", [1, 2 + TILES], I32)
        ident = sb("ident", [P, P])
        iota = sb("iota", [P, W])
        spare = sb("spare", [1, 32], I32)
        ones = sb("ones", [1, P])
        vw = sb("vw", [P, 5 * 12])
        arena = sb("arena", [P, 5224])
        used = [0]

        def carve(shape, dt=F32):
            size = int(np.prod(shape[1:]))
            a = arena[0:shape[0], used[0]:used[0] + size]
            used[0] += size
            assert used[0] <= 5224, used[0]
            if len(shape) == 3:
                a = a.rearrange("p (a b) -> p a b", b=shape[2])
            return a

        one_a = carve([P, 2, P])
        one_t = carve([P, 2, P])
        one_b = carve([P, 2, P])
        sw = carve([P, 2, GT * 6 * W])
        bblk = carve([P, 2, 64])
        mask = carve([96, 2, 257])
        joins = carve([1, 2, 32])
        sc = carve([P, 96])
        scl = carve([P, 96])
        fsc = carve([96, P])
        mseg = carve([96, P])
        mrun = carve([96, P])
        expo = carve([96, P])
        wT = carve([96, P])
        wE = carve([P, 2, 96])
        lm = carve([P, 2, P])
        fac = carve([P, 2, 96])
        fdg = carve([12, 96])
        facT = carve([12, 2, 16])
        tmp = carve([P, 2, 12])
        qrow = carve([1, 4 * 17])
        arow = carve([1, 4 * 17])
        urow = carve([1, 4 * 17])
        vrow = carve([1, 96])
        rrow = carve([1, 96])
        xrow = carve([1, 96])
        frow = carve([1, 96])
        used[0] = 0
        t1 = carve([P, 768])
        t2 = carve([P, 768])
        xT = carve([P, 256])
        xo = carve([P, 2, 262])
        bo = carve([P, 2, 6])
        xoT = carve([P, 256])
        tsum = carve([P, 256])
        tmin = carve([P, 256])
        texp = carve([P, 256])
        trel = carve([P, 256])
        dmb = carve([12, P])
        scal = carve([P, 64])
        x0 = carve([P, 2, P])
        red = carve([P, P])
        bias = carve([P, 512])

        ps = [ctx.enter_context(nc.psum_tensor(f"ps{i}", [P, 512], F32)) for i in range(8)]

        def g_rows(l):
            t = acc[:, 8 * NP:8 * NP + 2 * l.CT * l.ROW] if l.number == 1 else ring[:, 0:2 * l.CT * l.ROW]
            return t.rearrange("p (s c) -> p s c", c=l.ROW)

        def sums(l):
            return acc[:, 0:l.Q * NP].rearrange("p (q n) -> p q n", n=NP)

        ab = ring[:, 0:1536]
        wts = ring[:, 1536:1536 + 1792]
        xin = ring[:, 3328:3328 + 2 * 262].rearrange("p (s c) -> p s c", c=262)
        bin_ = ring[:, 3856:3856 + 12].rearrange("p (s c) -> p s c", c=6)

        def prep(k, width=512, dt=F32):
            a = ring[0:TG, k * 512:k * 512 + NG4 * (width // 4)]
            if dt is I32:
                a = a.bitcast(I32)
            return a.rearrange("p (g e) -> p g e", g=NG4)

        srcR, dstR = prep(0, dt=I32), prep(1, dt=I32)
        srcF, dstF, lastR = prep(2), prep(3), prep(4)
        mt = prep(5, width=4 * 257)
        rows4 = acc[0:1, 8 * NP:8 * NP + 4 * TILES].rearrange("p (k t) -> p k t", t=TILES)
        dstE = ring[:, 3600:3600 + TILES]
        iotaI = ring[:, 4032:4032 + W].bitcast(I32)
        tail = 12 * NP - 5632
        wofs, aofs, o = [], [], tail
        for l in LAYERS:
            wofs.append(o)
            o += l.ND * l.HC
        for l in LAYERS:
            aofs.append(o)
            o += 2 * l.HC
        prod = acc[:, o:o + 768]
        assert o + 768 <= 12 * NP

        def vvec(l):
            o = (0, 12, 36)[l.number]
            return vw[:, o:o + l.ND * 2 * l.H].rearrange("p (d h) -> p d h", h=2 * l.H)

        block = ctx.enter_context(nc.Block())

        CREDIT = {"turned": 8, "turned_used": 8, "turned_copied": 8, "expo_ready": 2, "summed": 32,
                  "window": 8, "merged": 8, "row_out0": 16, "row_out1": 16, "scores_out": 2,
                  "block_done": 2, "heads_done": 2, "skip_done": 2, "row_scored": 2, "x_copied": 2, "rows0": 16, "rows1": 16}

        def after(name, count):
            return CREDIT.get(name, 0) + count

        def give(eng, *names):
            for name in names:
                eng.sem_inc(sem(name), CREDIT[name])

        def give_dma(eng, at, *names):
            for k, name in enumerate(names):
                eng.dma_start(spare[0:1, at + 8 * k:at + 8 * k + 8],
                              src[0:8].unsqueeze(0)).then_inc(sem(name), CREDIT[name])

        def hold(eng, name):
            eng.sem_inc(sem("held_" + name), 1)

        def chunks(eng, l, chunk):
            half = l.CHUNKS // 2
            chunk(0, 0, 0, True)
            chunk(1, 0, 1, True)
            with eng.Fori(1, half - 1) as i:
                chunk(2 * i, i, 0, True)
                chunk(2 * i + 1, i, 1, True)
            chunk(l.CHUNKS - 2, half - 1, 0, True)
            chunk(l.CHUNKS - 1, half - 1, 1, False)

        def first_chunk(c):
            return isinstance(c, int) and c == 0

        def following(c, pair, par):
            return c + 1, pair + par, 1 - par

        def blocks(eng, block_of):
            with eng.Fori(0, NB // 2) as i:
                block_of(2 * i, i, 0)
                block_of(2 * i + 1, i, 1)
            block_of(NB - 1, NB // 2, 0)

        STEP_SLOTS = {
            16: {"pe": (0, 2, 4, 5, 7, 9, 11), "dve": (0, 1, 5, 6, 8, 10, 12), "act": (1, 3, 9, 10, 12)},
            8: {"pe": (0, 1, 3, 4, 5, 6), "dve": (0, 3, 4, 5, 6, 7), "act": (1, 5, 6, 7)},
        }
        ACT_LAG, DVE_LAG = 1, 2

        def due(engine, CT, t):
            return [k for k, at in enumerate(STEP_SLOTS[CT][engine]) if at == t]

        def bases(eng, l, c, lag=0):
            _, values = nc.values_load_multi_w_load_instructions(
                baseI[0:1, bass.ds(c * l.CT + DVE_LAG - lag, l.CT)], engines=[eng.engine], min_val=0, max_val=N - 1,
                skip_runtime_bounds_check_because="destinations are node numbers")
            return values

        SLOT0 = [16 * l.number * TILES // 2 for l in LAYERS]
        MASKS = [l.H + 2 for l in LAYERS]
        MASK0 = [0, 13 * MASKS[0], 13 * (MASKS[0] + MASKS[1])]
        PAIRS = (NB - NB // 2, NB // 2)
        DEPS = (11, 11, 17)

        def lm_of(l, par):
            return lm[:, par, 0:l.CT * 2 * l.H].rearrange("p (t k) -> p t k", k=2 * l.H)

        def pairs_before(l, c, g):
            return l.group0 // 2 + c * (l.GROUPS // 2) + g // 2

        def agg_done(eng, l):
            eng.wait_ge(sem("window"), after("window", 2 * (l.tile0 + TILES)))
            eng.wait_ge(sem("merged"), after("merged", 2 * (l.tile0 + TILES)))

        @block.sync
        def _(sp):
            give_dma(sp, 0, "row_out0", "row_out1")
            sp.wait_ge(sem("pad_set"), 2)
            for rows, arr in ((srcR, src), (dstR, dst)):
                whole = 3 * TG * P
                left = E - whole
                sp.dma_start(rows[:, 0:3, :], arr[0:whole].rearrange("(g p e) -> p g e", g=3, p=TG)).then_inc(sem("edges_in"), 16)
                sp.dma_start(rows[0:left // P, 3, :], arr[whole:whole + left // P * P].rearrange("(p e) -> p e", e=P)).then_inc(sem("edges_in"), 16)
                sp.dma_start(rows[left // P:left // P + 1, 3, 0:left % P],
                             arr[whole + left // P * P:E].rearrange("(p e) -> p e", p=1)).then_inc(sem("edges_in"), 16)
            for l, o, a in zip(LAYERS, wofs, aofs):
                p = params[l.number]
                sp.dma_start(acc[:, o:o + l.ND * l.HC].rearrange("p (d c) -> p d c", c=l.HC),
                             p["W"].rearrange("(d p) c -> p d c", p=P)).then_inc(sem("weights_in"), 16)
                for k, name in enumerate(("as", "ad")):
                    row = p[name].rearrange("h c -> (h c)").unsqueeze(0).broadcast_to([P, l.HC])
                    sp.dma_start(acc[:, a + k * l.HC:a + (k + 1) * l.HC], row).then_inc(sem("weights_in"), 16)
            sp.wait_ge(sem("masks_made"), 3)
            sp.dma_start(masks_d.rearrange("(g p) c -> p g c", p=TG), mt).then_inc(sem("masks_out"), 16)
            sp.wait_ge(sem("joins_made"), 1)
            sp.dma_start(joins_d.rearrange("k t -> (k t)").unsqueeze(0), rows4[:, 2:4, :].rearrange("p k t -> p (k t)")).then_inc(sem("masks_out"), 16)

            def load_tile_scores(l, c, pair, par):
                first = bases(sp, l, c)
                g1 = l.group0 + c * l.GROUPS
                n1 = CHUNK0[l.number] + c + 1
                sp.wait_ge(sem("turned_used"), after("turned_used", g1 - l.GROUPS))
                hold(sp, "sp")
                sp.wait_ge(sem("expo_ready"), after("expo_ready", n1 - 2))
                hold(sp, "sp")
                for t in range(l.CT):
                    j = t % GT
                    sp.dma_start(bblk[j * W:(j + 1) * W, par, t * l.H:(t + 1) * l.H],
                                 dtable[l.number][bass.ds(first[t], W), :]).then_inc(sem(f"bwin{par}"), 16)
                for h in range(l.H):
                    sp.dma_start(mask[h * l.CT:(h + 1) * l.CT, par, :],
                                 masks_d[bass.ds(c * l.CT, l.CT), :]).then_inc(sem(f"mask{par}"), 16)
                for k in range(2):
                    sp.dma_start(joins[0:1, par, k * l.CT:(k + 1) * l.CT],
                                 joins_d[k:k + 1, bass.ds(c * l.CT, l.CT)]).then_inc(sem(f"mask{par}"), 16)

            def load_block(l, k, pair, par):
                eb = NB * l.number + k
                sp.wait_ge(sem("block_done"), after("block_done", eb + 1 - 2))
                hold(sp, "sp")
                sp.dma_start(xin[:, par, 0:l.ROW], table[l.number][bass.ds(k * P, P), :]).then_inc(sem(f"block_in{par}"), 16)
                sp.dma_start(bin_[:, par, 0:l.H], dtable[l.number][bass.ds(k * P, P), :]).then_inc(sem(f"block_in{par}"), 16)
                sp.dma_start(x0[:, par, :], table[0][bass.ds(k * P, P), 0:P]).then_inc(sem(f"block_in{par}"), 16)

            def store_rows(s, k, pair, par):
                l = LAYERS[s]
                sp.wait_ge(sem("scores_out"), after("scores_out", 2 * (NB * s + k + 1)))
                hold(sp, "sp")
                sp.dma_start(table[s][bass.ds(k * P, P), :], xo[:, par, 0:l.ROW]).then_inc(sem(f"row_out{par}"), 16)
                sp.dma_start(dtable[s][bass.ds(k * P, P), :], bo[:, par, 0:l.H]).then_inc(sem(f"row_out{par}"), 16)

            def store_out(k, par, rows):
                sp.wait_ge(sem("block_done"), after("block_done", NB * 2 + k + 1))
                hold(sp, "sp")
                sp.dma_start(out[bass.ds(k * P, rows), :], xo[0:rows, par, 0:P]).then_inc(sem(f"out{par}"), 16)

            def load_input(k, pair, par, rows=P):
                sp.wait_ge(sem(f"row_out{par}"), after(f"row_out{par}", 32 * pair))
                hold(sp, "sp")
                sp.dma_start(xo[0:rows, par, 0:P], x[bass.ds(k * P, rows), :]).then_inc(sem(f"input{par}"), 16)

            load_input(0, 0, 0)
            with sp.Fori(0, NB // 2 - 1) as i:
                load_input(2 * i + 1, i, 1)
                store_rows(0, 2 * i, i, 0)
                load_input(2 * i + 2, i + 1, 0)
                store_rows(0, 2 * i + 1, i, 1)
            load_input(NB - 2, NB // 2 - 1, 1)
            store_rows(0, NB - 3, NB // 2 - 1, 0)
            sp.wait_ge(sem("last_rows_zero"), 1)
            load_input(NB - 1, NB // 2, 0, rows=N - (NB - 1) * P)
            store_rows(0, NB - 2, NB // 2 - 1, 1)
            store_rows(0, NB - 1, NB // 2, 0)

            for l in LAYERS:
                s = l.number
                sp.wait_ge(sem("masks_out"), 32)
                sp.wait_ge(sem("layer_clear"), s + 1)
                for par in range(2):
                    sp.wait_ge(sem(f"row_out{par}"), after(f"row_out{par}", 32 * PAIRS[par] * (s + 1)))
                sp.wait_ge(sem("bases_made"), 1)
                load_tile_scores(l, 0, 0, 0)

                def chunk(c, pair, par, more):
                    if more:
                        load_tile_scores(l, *following(c, pair, par))
                chunks(sp, l, chunk)

                agg_done(sp, l)
                p = params[s]
                sp.dma_start(wts[:, 0:l.ND * l.HC].rearrange("p (d c) -> p d c", c=l.HC),
                             p["W"].rearrange("(d p) c -> p d c", p=P)).then_inc(sem("wts_in"), 16)
                sp.dma_start(wts[:, l.ND * l.HC:l.ND * (l.HC + l.OUT)].rearrange("p (d c) -> p d c", c=l.OUT),
                             p["sW"].rearrange("(d p) c -> p d c", p=P)).then_inc(sem("wts_in"), 16)
                for k, name in enumerate(("b", "sb")):
                    sp.dma_start(bias[:, k * l.OUT:(k + 1) * l.OUT],
                                 p[name].unsqueeze(0).broadcast_to([P, l.OUT])).then_inc(sem("wts_in"), 16)
                load_block(l, 0, 0, 0)
                with sp.Fori(0, NB // 2) as i:
                    load_block(l, 2 * i + 1, i, 1)
                    if s < 2:
                        store_rows(s + 1, 2 * i, i, 0)
                    else:
                        store_out(2 * i, 0, P)
                    load_block(l, 2 * i + 2, i + 1, 0)
                    if s < 2:
                        store_rows(s + 1, 2 * i + 1, i, 1)
                    else:
                        store_out(2 * i + 1, 1, P)
                if s < 2:
                    store_rows(s + 1, NB - 1, NB // 2, 0)
                else:
                    store_out(NB - 1, 0, N - (NB - 1) * P)
            for par in range(2):
                sp.wait_ge(sem(f"out{par}"), 16 * PAIRS[par])

        @block.gpsimd
        def _(pool):
            give_dma(pool, 16, "rows0", "rows1")
            pool.memset(ident[:, :], 0.0).then_inc(sem("ident_zero"), 1)
            pool.wait_ge(sem("ident_zero"), 1)
            pool.affine_select(out=ident[:, :], in_=ident[:, :], compare_op=ALU.not_equal, fill=1.0, base=0,
                               pattern=[[-1, P]], channel_multiplier=1).then_inc(sem("ident"), 1)
            pool.iota(iotaI, pattern=[[1, W]], base=0, channel_multiplier=0).then_inc(sem("iota"), 1)
            pool.memset(acc[:, 0:4 * NP], 0.0).then_inc(sem("sums_zero"), 1)
            pool.memset(dm[:, :], 0.0).then_inc(sem("sums_zero"), 1)
            pool.wait_ge(sem("idx_made"), 1)
            pool.wait_ge(sem("joins_made"), 1)
            pool.wait_ge(sem("masks_out"), 32)

            for l in LAYERS:
                s = l.number
                rows = g_rows(l)
                for par in range(2):
                    pool.wait_ge(sem(f"row_out{par}"), after(f"row_out{par}", 32 * PAIRS[par] * (s + 1)))
                hold(pool, "pool")

                def gather(c, pair, par, more):
                    n = CHUNK0[s] + c
                    T = l.tile0 + c * l.CT
                    pool.wait_ge(sem(f"rows{par}"), after(f"rows{par}", SLOT0[s] + 16 * l.CT * pair))
                    hold(pool, "pool")
                    pool.tensor_copy(islot[:, par, 0:l.CT], idx[:, bass.ds(c * l.CT, l.CT)]).then_inc(sem("islot"), 1)
                    pool.wait_ge(sem("islot"), n + 1)
                    for t in range(l.CT):
                        pool.wait_ge(sem("summed"), after("summed", T - 2 * l.CT + t + 1))
                        hold(pool, "pool")
                        pool.indirect_dma_start(
                            out=rows[:, par * l.CT + t, :], out_offset=None, in_=table[s],
                            in_offset=bass.IndirectOffsetOnAxis(ap=islot[:, par, t:t + 1], axis=0)
                        ).then_inc(sem(f"rows{par}"), 16)
                chunks(pool, l, gather)

                agg_done(pool, l)
                hold(pool, "pool")

                def copy_block(k, pair, par):
                    eb = NB * s + k
                    pool.wait_ge(sem("heads_done"), after("heads_done", eb))
                    hold(pool, "pool")
                    pool.tensor_copy(ab[:, 0:l.Q // 2 * P].rearrange("p (q n) -> p q n", n=P),
                                     sums(l)[:, 0:l.Q // 2, bass.ds(k * P, P)]).then_inc(sem("half_copied"), 1)
                blocks(pool, copy_block)

        @block.scalar
        def _(act):
            give(act, "turned_copied", "window", "x_copied")
            def rows_turned(s, k, pair, par):
                l = LAYERS[s]
                tb = NB * s + k
                act.wait_ge(sem("row_turned"), tb + 1)
                act.wait_ge(sem("row_scored"), after("row_scored", tb))
                nc.scalar.activation(xoT[:, 0:l.D], ps[5][:, 0:l.D], ACT.Copy).then_inc(sem("row_copied"), 1)

            blocks(act, lambda k, pair, par: rows_turned(0, k, pair, par))

            for l in LAYERS:
                s = l.number
                HT = l.HT
                act.wait_ge(sem("bases_made"), 1)

                def score_step(step, c, pair, par):
                    n = CHUNK0[s] + c
                    halves = l.GROUPS // 2
                    if step < halves:
                        gg = l.group0 + c * l.GROUPS + 2 * step
                        act.wait_ge(sem("turned"), after("turned", gg + 2))
                        act.wait_ge(sem("turned_used"), after("turned_used", gg))
                        nc.scalar.activation(one_t, ps[4][:, 0:2 * P].rearrange("p (g e) -> p g e", e=P),
                                             ACT.Copy).then_inc(sem("turned_copied"), 1)
                    elif step == halves:
                        act.wait_ge(sem("chain_gap"), n + 1)
                        nc.scalar.activation(frow[:, 0:HT], xrow[:, 0:HT], ACT.Exp).then_inc(sem("factor"), 1)
                    elif step == halves + 1:
                        act.wait_ge(sem("expo_ready"), after("expo_ready", n + 1))
                        nc.scalar.activation(wT[0:HT, :], expo[0:HT, :], ACT.Exp).then_inc(sem("wT"), 1)
                    else:
                        act.wait_ge(sem("weights_turned"), 2 * (n + 1))
                        nc.scalar.activation(wE[:, par, 0:HT], ps[6][:, 128:128 + HT], ACT.Copy).then_inc(sem("weights"), 1)
                        nc.scalar.activation(lm_of(l, par)[:, :, 0:l.H], ps[6][:, 128:128 + HT].rearrange("p (h t) -> p t h", h=l.H),
                                             ACT.Copy).then_inc(sem("weights"), 1)

                steps = l.GROUPS // 2 + 3
                for k in range(steps):
                    score_step(k, 0, 0, 0)

                def window(T, t, at):
                    z = ps[t % 4]
                    act.wait_ge(sem("summed"), after("summed", T + 1))
                    act.wait_ge(sem("window"), after("window", 2 * T))
                    hold(act, "act")
                    nc.scalar.activation(sums(l)[:, :, bass.ds(at + 1, W - 1)],
                                         z[:, 0:l.QW].rearrange("p (q w) -> p q w", w=W)[:, :, 1:W],
                                         ACT.Copy).then_inc(sem("window"), 1)
                    nc.scalar.activation(dm[0:2 * l.H, bass.ds(at + 1, W - 1)], z[0:2 * l.H, 417:417 + W - 1],
                                         ACT.Copy).then_inc(sem("window"), 1)

                def chunk(c, pair, par, more):
                    first = bases(act, l, c, ACT_LAG)
                    for t in range(l.CT):
                        if not (first_chunk(c) and t < ACT_LAG):
                            window(l.tile0 + c * l.CT + t - ACT_LAG, (t - ACT_LAG) % l.CT, first[t])
                        if more:
                            for k in due("act", l.CT, t):
                                score_step(k, *following(c, pair, par))
                    if not more:
                        last = bases(act, l, l.CHUNKS - 1)
                        window(l.tile0 + TILES - 1, l.CT - 1, last[-1])
                chunks(act, l, chunk)

                agg_done(act, l)
                hold(act, "act")

                def finish_block(k, pair, par):
                    eb = NB * s + k
                    act.wait_ge(sem("heads_done"), after("heads_done", eb))
                    hold(act, "act")
                    nc.scalar.activation(ab[:, l.Q // 2 * P:l.Q * P].rearrange("p (q n) -> p q n", n=P),
                                         sums(l)[:, l.Q // 2:l.Q, bass.ds(k * P, P)], ACT.Copy).then_inc(sem("half_copied"), 1)
                    act.wait_ge(sem("x_turned"), eb + 1)
                    act.wait_ge(sem("skip_done"), after("skip_done", eb))
                    nc.scalar.activation(xT[:, 0:l.D], ps[4][:, 0:l.D], ACT.Copy).then_inc(sem("x_copied"), 1)
                    act.wait_ge(sem("gaps"), eb + 1)
                    nc.scalar.activation(scal[:, 12:12 + 2 * l.H], scal[:, 0:2 * l.H], ACT.Exp).then_inc(sem("exp2"), 1)
                    act.wait_ge(sem("preact"), eb + 1)
                    nc.scalar.activation(trel[:, 0:l.OUT], tsum[:, 0:l.OUT], ACT.Relu).then_inc(sem("elu"), 1)
                    act.wait_ge(sem("negative"), eb + 1)
                    nc.scalar.activation(texp[:, 0:l.OUT], tmin[:, 0:l.OUT], ACT.Exp).then_inc(sem("elu"), 1)
                    if s < 2:
                        rows_turned(s + 1, k, pair, par)
                    else:
                        act.wait_ge(sem("variance"), k + 1)
                        nc.scalar.activation(scal[:, 50:51], scal[:, 49:50], ACT.Sqrt).then_inc(sem("deviation"), 1)
                blocks(act, finish_block)

        @block.tensor
        def _(pe):
            give(pe, "turned", "turned_used", "summed", "heads_done", "skip_done", "row_scored")
            pe.wait_ge(sem("ident"), 1)
            for k, (name, rows) in enumerate((("dst_float", dstF), ("src_float", srcF), ("last_made", lastR))):
                pe.wait_ge(sem(name), 1)
                for g in range(NG4):
                    nc.tensor.transpose(ps[k][:, g * TG:(g + 1) * TG], rows[:, g, :], ident[0:TG, 0:TG]).then_inc(sem("edges_turned"), 1)
            pe.wait_ge(sem("ones"), 1)
            pe.wait_ge(sem("dstE"), 1)
            nc.tensor.matmul(ps[3][:, 0:TILES], lhsT=ones[0:1, :], rhs=dstE[0:1, :], start=True, stop=True).then_inc(sem("firsts"), 1)
            nc.tensor.matmul(ps[6][0:1, 0:TILES], lhsT=ident[:, P - 1:P], rhs=dstE, start=True, stop=True).then_inc(sem("firsts"), 1)
            pe.wait_ge(sem("vectors"), 10)

            def row_scores(s, k, pair, par):
                l = LAYERS[s]
                tb = NB * s + k
                if s == 0:
                    pe.wait_ge(sem(f"input{par}"), 16 * (pair + 1))
                else:
                    pe.wait_ge(sem("features"), NB * (s - 1) + k + 1)
                for d in range(l.ND):
                    last = nc.tensor.transpose(ps[5][:, d * P:(d + 1) * P], xo[:, par, d * P:(d + 1) * P], ident[:, :])
                last.then_inc(sem("row_turned"), 1)
                pe.wait_ge(sem("row_copied"), tb + 1)
                pe.wait_ge(sem("scores_out"), after("scores_out", 2 * tb))
                for d in range(l.ND):
                    last = nc.tensor.matmul(ps[7][:, 0:2 * l.H], lhsT=xoT[:, d * P:(d + 1) * P], rhs=vvec(l)[:, d, :],
                                            start=d == 0, stop=d == l.ND - 1)
                last.then_inc(sem("row_scored"), 1)

            blocks(pe, lambda k, pair, par: row_scores(0, k, pair, par))

            for l in LAYERS:
                s, H, CT, HT = l.number, l.H, l.CT, l.HT
                rows = g_rows(l)

                def turn(c, g):
                    gg = l.group0 + c * l.GROUPS + g
                    pe.wait_ge(sem("turned_copied"), after("turned_copied", pairs_before(l, c, g)))
                    for k in range(2):
                        pe.wait_ge(sem("onehot_a"), gg + k + 1)
                        nc.tensor.transpose(ps[4][:, k * P:k * P + P], one_a[:, k, :], ident[:, :]).then_inc(sem("turned"), 1)

                def expand(c, pair, par, g):
                    gg = l.group0 + c * l.GROUPS + g
                    if g % 2 == 0:
                        pe.wait_ge(sem("turned_copied"), after("turned_copied", pairs_before(l, c, g) + 1))
                    if g == 0:
                        pe.wait_ge(sem(f"bwin{par}"), SLOT0[s] + 16 * CT * (pair + 1))
                    nc.tensor.matmul(ps[5][:, g * GT * H:(g + 1) * GT * H], lhsT=one_t[:, g % 2, :],
                                     rhs=bblk[:, par, g * GT * H:(g + 1) * GT * H], start=True, stop=True).then_inc(sem("turned_used"), 1)

                half = l.GROUPS // 2
                steps = half + 5

                def score_step(step, c, pair, par):
                    n = CHUNK0[s] + c
                    if step <= half:
                        if step:
                            expand(c, pair, par, 2 * step - 2)
                            expand(c, pair, par, 2 * step - 1)
                        if step < half:
                            turn(c, 2 * step)
                    elif step == half + 1:
                        pe.wait_ge(sem("scored"), n + 1)
                        hold(pe, "pe")
                        nc.tensor.transpose(ps[6][0:HT, 0:P], scl[:, 0:HT], ident[:, :]).then_inc(sem("score_turned"), 1)
                    elif step == half + 2:
                        pe.wait_ge(sem("segmax"), n + 1)
                        hold(pe, "pe")
                        nc.tensor.transpose(ps[7][0:1, 0:HT], mseg[0:HT, 0:1], ident[0:HT, 0:HT]).then_inc(sem("ends"), 1)
                        nc.tensor.transpose(ps[7][0:1, 128:128 + HT], mseg[0:HT, P - 1:P], ident[0:HT, 0:HT]).then_inc(sem("ends"), 1)
                    elif step == half + 3:
                        pe.wait_ge(sem("running"), n + 1)
                        nc.tensor.matmul(ps[7][0:HT, 256:257], lhsT=rrow[:, 0:HT], rhs=ones[0:1, 0:1], start=True, stop=True).then_inc(sem("spread"), 1)
                        pe.wait_ge(sem("factor"), n + 1)
                        nc.tensor.matmul(ps[7][:, 384:384 + HT], lhsT=ones[0:1, :], rhs=frow[:, 0:HT], start=True, stop=True).then_inc(sem("spread"), 1)
                    else:
                        pe.wait_ge(sem("wT"), n + 1)
                        hold(pe, "pe")
                        nc.tensor.transpose(ps[7][:, 0:HT], mrun[0:HT, :], ident[0:HT, 0:HT]).then_inc(sem("weights_turned"), 1)
                        nc.tensor.transpose(ps[6][:, 128:128 + HT], wT[0:HT, :], ident[0:HT, 0:HT]).then_inc(sem("weights_turned"), 1)

                for k in range(steps):
                    score_step(k, 0, 0, 0)

                def chunk(c, pair, par, more):
                    for t in range(CT):
                        T = l.tile0 + c * CT + t
                        g = t // GT
                        z = ps[t % 4]
                        pe.wait_ge(sem("weighted"), T + 1)
                        if t == 0:
                            pe.wait_ge(sem("weights"), 2 * (CHUNK0[s] + c + 1))
                            pe.wait_ge(sem("last_max"), CHUNK0[s] + c + 1)
                        pe.wait_ge(sem("window"), after("window", 2 * (T - 3)))
                        pe.wait_ge(sem("merged"), after("merged", 2 * (T - 3)))
                        w = sw[:, g % 2, t % GT * H * W:(t % GT + 1) * H * W]
                        for d in range(l.ND):
                            nc.tensor.matmul(z[:, d * H * W:(d + 1) * H * W], lhsT=rows[:, par * CT + t, d * P:(d + 1) * P],
                                             rhs=w, start=True, stop=True)
                        nc.tensor.matmul(z[0:2 * H, 416:416 + W], lhsT=lm[:, par, t * 2 * H:(t + 1) * 2 * H],
                                         rhs=one_b[:, g % 2, t % GT * W:(t % GT + 1) * W], start=True, stop=True).then_inc(sem("summed"), 1)
                        if more:
                            for k in due("pe", CT, t):
                                score_step(k, *following(c, pair, par))
                chunks(pe, l, chunk)

                agg_done(pe, l)
                pe.wait_ge(sem("wts_in"), 64 * (s + 1))
                Wv = wts[:, 0:l.ND * l.HC].rearrange("p (d c) -> p d c", c=l.HC)
                sWv = wts[:, l.ND * l.HC:l.ND * (l.HC + l.OUT)].rearrange("p (d c) -> p d c", c=l.OUT)

                def finish_block(k, pair, par):
                    eb = NB * s + k
                    pe.wait_ge(sem(f"block_in{par}"), 48 * (PAIRS[par] * s + pair + 1))
                    pe.wait_ge(sem("x_copied"), after("x_copied", eb))
                    for d in range(l.ND):
                        last = nc.tensor.transpose(ps[4][:, d * P:(d + 1) * P], xin[:, par, d * P:(d + 1) * P], ident[:, :])
                    last.then_inc(sem("x_turned"), 1)
                    pe.wait_ge(sem("dm_copied"), eb + 1)
                    hold(pe, "pe")
                    nc.tensor.transpose(ps[6][:, 0:2 * H], dmb[0:2 * H, :], ident[0:2 * H, 0:2 * H]).then_inc(sem("dm_turned"), 1)
                    pe.wait_ge(sem("half_copied"), 2 * (eb + 1))
                    pe.wait_ge(sem("block_done"), after("block_done", eb))
                    for h in range(H):
                        at = h * l.C
                        for d in range(l.ND):
                            last = nc.tensor.matmul(ps[at // 512][:, at % 512:at % 512 + l.C], lhsT=ab[:, (d * H + h) * P:(d * H + h + 1) * P],
                                                    rhs=Wv[:, d, at:at + l.C], start=d == 0, stop=d == l.ND - 1)
                    last.then_inc(sem("heads_done"), 1)
                    pe.wait_ge(sem("x_copied"), after("x_copied", eb + 1))
                    for at in range(0, l.HC, 512):
                        n = min(512, l.HC - at)
                        for d in range(l.ND):
                            nc.tensor.matmul(ps[2 + at // 512][:, 0:n], lhsT=xT[:, d * P:(d + 1) * P], rhs=Wv[:, d, at:at + n],
                                             start=d == 0, stop=d == l.ND - 1)
                    for d in range(l.ND):
                        last = nc.tensor.matmul(ps[1][:, 256:256 + l.OUT], lhsT=xT[:, d * P:(d + 1) * P], rhs=sWv[:, d, :],
                                                start=d == 0, stop=d == l.ND - 1)
                    last.then_inc(sem("skip_done"), 1)
                    if s < 2:
                        row_scores(s + 1, k, pair, par)
                blocks(pe, finish_block)

        @block.vector
        def _(v):
            step = [0]

            def link(ins):
                step[0] += 1
                ins.then_inc(sem("prep_step"), 1)
                v.wait_ge(sem("prep_step"), step[0])

            give(v, "expo_ready", "merged", "scores_out", "block_done")
            v.memset(srcR[:, 3, :], 0).then_inc(sem("pad_set"), 1)
            v.memset(dstR[:, 3, :], N).then_inc(sem("pad_set"), 1)
            v.memset(ones[:, :], 1.0).then_inc(sem("ones"), 1)
            v.memset(vrow[:, :], 0.0)
            v.memset(arow[:, :], -BIG)
            link(v.memset(urow[:, :], 0.0))
            v.wait_ge(sem("edges_in"), 96)
            v.tensor_copy(dstF, dstR).then_inc(sem("dst_float"), 1)
            v.tensor_copy(srcF, srcR).then_inc(sem("src_float"), 1)
            v.wait_ge(sem("dst_float"), 1)
            link(v.memset(lastR[:, :, P - 1:P], 1.0))
            v.tensor_tensor(lastR[:, :, 0:P - 1], dstF[:, :, 0:P - 1], dstF[:, :, 1:P], ALU.not_equal).then_inc(sem("last_made"), 1)
            v.memset(mt[:, :, 0:1], -BIG).then_inc(sem("masks_made"), 1)
            v.memset(mt[:, :, P:P + 1], -BIG).then_inc(sem("masks_made"), 1)
            link(v.tensor_tensor(mt[:, :, P + 1:2 * P + 1], dstF, dstF[:, :, 0:1].broadcast_to([TG, NG4, P]), ALU.not_equal))
            link(v.tensor_scalar(mt[:, :, P + 1:2 * P + 1], mt[:, :, P + 1:2 * P + 1], -BIG, None, ALU.mult))
            v.wait_ge(sem("last_made"), 1)
            v.tensor_scalar(mt[:, :, 1:P], lastR[:, :, 0:P - 1], -BIG, None, ALU.mult).then_inc(sem("masks_made"), 1)
            v.wait_ge(sem("iota"), 1)
            link(v.tensor_copy(iota[:, :], iotaI))
            v.wait_ge(sem("edges_turned"), 12)
            v.tensor_copy(dstE, ps[0][:, 0:TILES]).then_inc(sem("dstE"), 1)
            v.tensor_copy(idx[:, :], ps[1][:, 0:TILES]).then_inc(sem("idx_made"), 1)
            link(v.tensor_copy(lastE[:, :], ps[2][:, 0:TILES]))
            v.wait_ge(sem("dstE"), 1)
            link(v.memset(baseI[:, 0:DVE_LAG], 0))
            v.tensor_copy(baseI[:, DVE_LAG:DVE_LAG + TILES], dstE[0:1, :]).then_inc(sem("bases_made"), 1)
            v.wait_ge(sem("firsts"), 2)
            link(v.tensor_tensor(dloc[:, :], dstE, ps[3][:, 0:TILES], ALU.subtract))
            link(v.tensor_copy(rows4[:, 0, :], ps[6][0:1, 0:TILES]))
            link(v.memset(rows4[:, 2, 0:1], 1.0))
            link(v.tensor_tensor(rows4[:, 2, 1:TILES], dstE[0:1, 1:TILES], rows4[:, 0, 0:TILES - 1], ALU.not_equal))
            link(v.tensor_tensor(rows4[:, 1, :], dstE[0:1, :], rows4[:, 0, :], ALU.not_equal))
            link(v.tensor_tensor(rows4[:, 3, :], rows4[:, 1, :], rows4[:, 2, :], ALU.add))
            v.tensor_scalar(rows4[:, 2:4, :], rows4[:, 2:4, :], -BIG, None, ALU.mult).then_inc(sem("joins_made"), 1)
            v.wait_ge(sem("weights_in"), 144)
            for l, o, a in zip(LAYERS, wofs, aofs):
                for k in range(2):
                    for d in range(l.ND):
                        v.tensor_tensor(prod[:, 0:l.HC], acc[:, o + d * l.HC:o + (d + 1) * l.HC],
                                        acc[:, a + k * l.HC:a + (k + 1) * l.HC], ALU.mult).then_inc(sem("vproduct"), 1)
                        v.wait_ge(sem("vproduct"), (0, 2, 6)[l.number] + k * l.ND + d + 1)
                        v.tensor_reduce(vvec(l)[:, d, k * l.H:(k + 1) * l.H], prod[:, 0:l.HC].rearrange("p (h c) -> p h c", c=l.C),
                                        axis=AX.X, op=ALU.add).then_inc(sem("vectors"), 1)
                        v.wait_ge(sem("vectors"), (0, 2, 6)[l.number] + k * l.ND + d + 1)
            v.memset(acc[:, 4 * NP:8 * NP], 0.0).then_inc(sem("sums_zero"), 1)

            def scores_out(s, k, pair, par):
                l = LAYERS[s]
                tb = NB * s + k
                v.wait_ge(sem("row_scored"), after("row_scored", tb + 1))
                if s == 0:
                    v.wait_ge(sem(f"row_out{par}"), after(f"row_out{par}", 32 * pair))
                v.tensor_copy(xo[:, par, l.D:l.ROW], ps[7][:, 0:l.H]).then_inc(sem("scores_out"), 1)
                v.tensor_copy(bo[:, par, 0:l.H], ps[7][:, l.H:2 * l.H]).then_inc(sem("scores_out"), 1)

            with v.Fori(0, NB // 2) as i:
                scores_out(0, 2 * i, i, 0)
                scores_out(0, 2 * i + 1, i, 1)
            v.wait_ge(sem("row_out0"), after("row_out0", 32 * (NB // 2)))
            v.memset(xo[:, 0, 0:P], 0.0).then_inc(sem("last_rows_zero"), 1)
            scores_out(0, NB - 1, NB // 2, 0)

            for l in LAYERS:
                s, H, CT, HT, C1 = l.number, l.H, l.CT, l.HT, l.CT + 1
                rows = g_rows(l)
                half = l.GROUPS // 2
                steps = half + 5
                by_head = lambda a: a.rearrange("p (h t) -> p h t", h=H)
                with_carry = lambda a: a[:, 0:H * C1].rearrange("p (h t) -> p h t", h=H)

                for par in range(2):
                    v.wait_ge(sem(f"row_out{par}"), after(f"row_out{par}", 32 * PAIRS[par] * (s + 1)))
                v.memset(arow[:, :], -BIG).then_inc(sem("carry_clear"), 1)
                v.memset(bblk[:, :, :], 0.0).then_inc(sem("layer_clear"), 1)
                v.wait_ge(sem("layer_clear"), s + 1)
                v.wait_ge(sem("bases_made"), 1)

                def onehot(c, g, buf, name):
                    v.tensor_tensor(buf[:, g % 2, :].rearrange("p (t w) -> p t w", w=W),
                                    wide(iota[:, :], 1, [P, GT, W]),
                                    wide(dloc[:, bass.ds(c * CT + g * GT, GT)], 2, [P, GT, W]),
                                    ALU.is_equal).then_inc(sem(name), 1)

                def score_step(step, c, pair, par):
                    n = CHUNK0[s] + c
                    if step < half:
                        for g in (2 * step, 2 * step + 1):
                            gg = l.group0 + c * l.GROUPS + g
                            if g % 2 == 0:
                                v.wait_ge(sem("turned"), after("turned", gg))
                            onehot(c, g, one_a, "onehot_a")
                    elif step == half:
                        v.wait_ge(sem("turned_used"), after("turned_used", l.group0 + (c + 1) * l.GROUPS))
                        v.wait_ge(sem(f"rows{par}"), after(f"rows{par}", SLOT0[s] + 16 * CT * (pair + 1)))
                        v.tensor_tensor(by_head(sc[:, 0:HT]), rows[:, par * CT:(par + 1) * CT, l.D:l.ROW].rearrange("p t h -> p h t"),
                                        ps[5][:, 0:HT].rearrange("p (t h) -> p h t", h=H), ALU.add).then_inc(sem("score_sum"), 1)
                        v.wait_ge(sem("score_sum"), n + 1)
                        v.scalar_tensor_tensor(out=scl[:, 0:HT], in0=sc[:, 0:HT], scalar=SLOPE, in1=sc[:, 0:HT],
                                               op0=ALU.mult, op1=ALU.max).then_inc(sem("scored"), 1)
                    elif step == half + 1:
                        v.wait_ge(sem("score_turned"), n + 1)
                        v.wait_ge(sem(f"mask{par}"), 16 * MASK0[s] + 16 * MASKS[s] * (pair + 1))
                        v.tensor_tensor_scan(fsc[0:HT, :], mask[0:HT, par, 0:P], ps[6][0:HT, 0:P], 0.0,
                                             ALU.add, ALU.max).then_inc(sem("forward"), 1)
                        v.wait_ge(sem("forward"), n + 1)
                        v.tensor_tensor_scan(mseg[0:HT, ::-1], mask[0:HT, par, P:0:-1], fsc[0:HT, ::-1], 0.0,
                                             ALU.add, ALU.max).then_inc(sem("segmax"), 1)
                    elif step == half + 2:
                        v.tensor_copy(with_carry(qrow)[:, :, 0:1], with_carry(urow)[:, :, CT:C1]).then_inc(sem("chain_in"), 1)
                        v.tensor_copy(with_carry(arow)[:, :, 1:C1], wide(joins[:, par, CT:2 * CT], 1, [1, H, CT])).then_inc(sem("chain_in"), 1)
                        v.wait_ge(sem("ends"), 2 * (n + 1))
                        v.tensor_copy(with_carry(qrow)[:, :, 1:C1], by_head(ps[7][0:1, 128:128 + HT])).then_inc(sem("chain_in"), 1)
                        v.wait_ge(sem("chain_in"), 3 * (n + 1))
                        v.tensor_tensor_scan(urow[:, 0:H * C1], arow[:, 0:H * C1], qrow[:, 0:H * C1], 0.0,
                                             ALU.add, ALU.max).then_inc(sem("chain"), 1)
                        v.wait_ge(sem("chain"), n + 1)
                        v.tensor_tensor(by_head(vrow[:, 0:HT]), with_carry(urow)[:, :, 0:CT], wide(joins[:, par, 0:CT], 1, [1, H, CT]),
                                        ALU.add).then_inc(sem("incoming"), 1)
                        v.wait_ge(sem("incoming"), n + 1)
                        v.tensor_tensor(rrow[:, 0:HT], vrow[:, 0:HT], ps[7][0:1, 0:HT], ALU.max).then_inc(sem("running"), 1)
                        v.wait_ge(sem("running"), n + 1)
                        v.tensor_tensor(xrow[:, 0:HT], vrow[:, 0:HT], rrow[:, 0:HT], ALU.subtract).then_inc(sem("chain_gap"), 1)
                    elif step == half + 3:
                        v.wait_ge(sem("spread"), 2 * (n + 1))
                        v.scalar_tensor_tensor(out=mrun[0:HT, :], in0=mask[0:HT, par, P + 1:2 * P + 1], scalar=ps[7][0:HT, 256:257],
                                               in1=mseg[0:HT, :], op0=ALU.add, op1=ALU.max).then_inc(sem("run_max"), 1)
                        v.tensor_copy(fac[:, par, 0:HT], ps[7][:, 384:384 + HT]).then_inc(sem("factors"), 1)
                        v.wait_ge(sem("run_max"), n + 1)
                        v.tensor_tensor(expo[0:HT, :], ps[6][0:HT, 0:P], mrun[0:HT, :], ALU.subtract).then_inc(sem("expo_ready"), 1)
                        v.wait_ge(sem("factors"), n + 1)
                        v.tensor_tensor(by_head(fdg[0:2 * H, 0:HT]), by_head(fac[0:2 * H, par, 0:HT]),
                                        wide(ident[0:2 * H, 0:H], 2, [2 * H, H, CT]), ALU.mult).then_inc(sem("own_factor"), 1)
                        v.wait_ge(sem("own_factor"), n + 1)
                        v.tensor_reduce(facT[0:2 * H, par, 0:CT], fdg[0:2 * H, 0:HT].rearrange("p (h t) -> p t h", h=H),
                                        axis=AX.X, op=ALU.add).then_inc(sem("head_factor"), 1)
                    else:
                        v.wait_ge(sem("weights_turned"), 2 * (n + 1))
                        v.tensor_tensor(lm_of(l, par)[:, :, H:2 * H], ps[7][:, 0:HT].rearrange("p (h t) -> p t h", h=H),
                                        wide(lastE[:, bass.ds(c * CT, CT)], 2, [P, CT, H]), ALU.mult).then_inc(sem("last_max"), 1)

                def weight(c, pair, par, g):
                    gg = l.group0 + c * l.GROUPS + g
                    v.wait_ge(sem("summed"), after("summed", GT * (gg - 1)))
                    onehot(c, g, one_b, "onehot_b")
                    if g == 0:
                        v.wait_ge(sem("weights"), 2 * (CHUNK0[s] + c + 1))
                    v.wait_ge(sem("onehot_b"), gg + 1)
                    for t in range(GT):
                        w = wE[:, par, 0:HT].rearrange("p (h t) -> p t h", h=H)[:, g * GT + t, :]
                        last = v.tensor_tensor(sw[:, g % 2, t * H * W:(t + 1) * H * W].rearrange("p (h w) -> p h w", w=W),
                                               wide(one_b[:, g % 2, t * W:(t + 1) * W], 1, [P, H, W]),
                                               wide(w, 2, [P, H, W]), ALU.mult)
                        last.then_inc(sem("weighted"), 1)

                for k in range(steps):
                    score_step(k, 0, 0, 0)
                weight(0, 0, 0, 0)

                def merge(T, t, par, at):
                    z = ps[t % 4]
                    v.wait_ge(sem("window"), after("window", 2 * T + 2))
                    v.wait_ge(sem("merged"), after("merged", 2 * T))
                    v.tensor_tensor(tmp[:, t % 2, 0:l.Q].rearrange("p (d h) -> p d h", h=H),
                                    sums(l)[:, :, bass.ds(at, 1)].rearrange("p (d h) o -> p d (h o)", h=H),
                                    wide(fac[:, par, 0:HT].rearrange("p (h t) -> p t h", h=H)[:, t, :], 1, [P, l.ND, H]),
                                    ALU.mult).then_inc(sem("kept"), 1)
                    v.scalar_tensor_tensor(out=dm[0:2 * H, bass.ds(at, 1)], in0=dm[0:2 * H, bass.ds(at, 1)],
                                           scalar=facT[0:2 * H, par, t:t + 1], in1=z[0:2 * H, 416:417],
                                           op0=ALU.mult, op1=ALU.add).then_inc(sem("merged"), 1)
                    v.wait_ge(sem("kept"), T + 1)
                    v.tensor_tensor(sums(l)[:, :, bass.ds(at, 1)].rearrange("p q o -> p (q o)"), tmp[:, t % 2, 0:l.Q],
                                    z[:, 0:l.QW].rearrange("p (q w) -> p q w", w=W)[:, :, 0], ALU.add).then_inc(sem("merged"), 1)

                def chunk(c, pair, par, more):
                    first = bases(v, l, c, DVE_LAG)
                    for t in range(CT):
                        if more:
                            for k in due("dve", CT, t):
                                score_step(k, *following(c, pair, par))
                        if t % GT == 0 and t // GT + 1 < l.GROUPS:
                            weight(c, pair, par, t // GT + 1)
                        if t == DVE_LAG:
                            v.wait_ge(sem("head_factor"), CHUNK0[s] + c + 1)
                        if not (first_chunk(c) and t < DVE_LAG):
                            merge(l.tile0 + c * CT + t - DVE_LAG, (t - DVE_LAG) % CT, par if t >= DVE_LAG else 1 - par, first[t])
                    if more:
                        c2, pair2, par2 = following(c, pair, par)
                        weight(c2, pair2, par2, 0)
                    else:
                        last = bases(v, l, l.CHUNKS - 1)
                        for t in range(CT - DVE_LAG, CT):
                            merge(l.tile0 + TILES - CT + t, t, par, last[t])
                chunks(v, l, chunk)

                agg_done(v, l)
                v.memset(sums(l)[:, :, N:NP], 0.0).then_inc(sem("pads"), 1)
                v.memset(dm[:, N:NP], 0.0).then_inc(sem("pads"), 1)
                v.wait_ge(sem("pads"), 2 * (s + 1))
                v.wait_ge(sem("wts_in"), 64 * (s + 1))
                v.tensor_tensor(bias[:, 0:l.OUT], bias[:, 0:l.OUT], bias[:, l.OUT:2 * l.OUT], ALU.add).then_inc(sem("bias_made"), 1)
                v.wait_ge(sem("bias_made"), s + 1)

                def finish_block(k, pair, par):
                    eb = NB * s + k
                    did = [0]

                    def dep(ins):
                        did[0] += 1
                        ins.then_inc(sem(f"finish{s}"), 1)
                        v.wait_ge(sem(f"finish{s}"), DEPS[s] * k + did[0])

                    v.tensor_copy(dmb[0:2 * H, :], dm[0:2 * H, bass.ds(k * P, P)]).then_inc(sem("dm_copied"), 1)
                    es, gap, e2, den, rden, r2, msx = (scal[:, 24:24 + H], scal[:, 0:2 * H], scal[:, 12:12 + 2 * H], scal[:, 30:30 + H],
                                                       scal[:, 30:30 + H], scal[:, 36:36 + 2 * H], scal[:, 52:52 + H])
                    v.wait_ge(sem(f"block_in{par}"), 48 * (PAIRS[par] * s + pair + 1))
                    dep(v.tensor_tensor(msx, xin[:, par, l.D:l.ROW], bin_[:, par, 0:H], ALU.add))
                    dep(v.scalar_tensor_tensor(out=es, in0=msx, scalar=SLOPE, in1=msx, op0=ALU.mult, op1=ALU.max))
                    v.wait_ge(sem("dm_turned"), eb + 1)
                    d_ps, m_ps = ps[6][:, 0:H], ps[6][:, H:2 * H]
                    dep(v.tensor_tensor(msx, es, m_ps, ALU.max))
                    v.tensor_tensor(gap[:, 0:H], m_ps, msx, ALU.subtract)
                    v.tensor_tensor(gap[:, H:2 * H], es, msx, ALU.subtract).then_inc(sem("gaps"), 1)
                    v.wait_ge(sem("exp2"), eb + 1)
                    dep(v.tensor_tensor(den, e2[:, 0:H], d_ps, ALU.mult))
                    dep(v.tensor_tensor(den, den, e2[:, H:2 * H], ALU.add))
                    dep(v.tensor_scalar(den, den, 1e-16, None, ALU.add))
                    dep(v.reciprocal(rden, den))
                    dep(v.tensor_tensor(r2.rearrange("p (k h) -> p k h", h=H), e2.rearrange("p (k h) -> p k h", h=H),
                                        wide(rden, 1, [P, 2, H]), ALU.mult))
                    v.wait_ge(sem("skip_done"), after("skip_done", eb + 1))
                    for at in range(0, l.HC, 512):
                        n = min(512, l.HC - at)
                        h0, hn = at // l.C, n // l.C
                        for out_, bank, r in ((t1, at // 512, r2[:, h0:h0 + hn]), (t2, 2 + at // 512, r2[:, H + h0:H + h0 + hn])):
                            last = v.tensor_tensor(out_[:, at:at + n].rearrange("p (h c) -> p h c", c=l.C),
                                                   ps[bank][:, 0:n].rearrange("p (h c) -> p h c", c=l.C),
                                                   wide(r, 2, [P, hn, l.C]), ALU.mult)
                            if out_ is t2 and at + n == l.HC:
                                dep(last)
                    if s < 2:
                        dep(v.tensor_tensor(t1[:, 0:l.HC], t1[:, 0:l.HC], t2[:, 0:l.HC], ALU.add))
                        dep(v.tensor_tensor(tsum[:, 0:l.OUT], t1[:, 0:l.OUT], ps[1][:, 256:256 + l.OUT], ALU.add))
                    else:
                        dep(v.tensor_tensor(t1[:, 0:l.HC], t1[:, 0:l.HC], t2[:, 0:l.HC], ALU.add))
                        dep(v.tensor_reduce(red[:, :], t1[:, 0:l.HC].rearrange("p (h c) -> p c h", c=l.C), axis=AX.X, op=ALU.add))
                        dep(v.scalar_tensor_tensor(out=tsum[:, 0:l.OUT], in0=red[:, :], scalar=1.0 / H,
                                                   in1=ps[1][:, 256:256 + l.OUT], op0=ALU.mult, op1=ALU.add))
                    v.tensor_tensor(tsum[:, 0:l.OUT], tsum[:, 0:l.OUT], bias[:, 0:l.OUT], ALU.add).then_inc(sem("preact"), 1)
                    v.wait_ge(sem("preact"), eb + 1)
                    v.tensor_scalar(tmin[:, 0:l.OUT], tsum[:, 0:l.OUT], 0.0, None, ALU.min).then_inc(sem("negative"), 1)
                    v.wait_ge(sem("elu"), 2 * (eb + 1))
                    if s < 2:
                        tb_pair = PAIRS[par] * (s + 1) + pair
                        v.wait_ge(sem(f"row_out{par}"), after(f"row_out{par}", 32 * tb_pair))
                        v.scalar_tensor_tensor(out=xo[:, par, 0:l.OUT], in0=texp[:, 0:l.OUT], scalar=-1.0, in1=trel[:, 0:l.OUT],
                                               op0=ALU.add, op1=ALU.add).then_inc(sem("features"), 1)
                        scores_out(s + 1, k, pair, par)
                        v.memset(scal[:, 58:59], 0.0).then_inc(sem("block_done"), 1)
                    else:
                        dep(v.scalar_tensor_tensor(out=red[:, :], in0=texp[:, 0:P], scalar=-1.0, in1=trel[:, 0:P],
                                                   op0=ALU.add, op1=ALU.add))
                        dep(v.tensor_tensor(t1[:, 0:P], red[:, :], x0[:, par, :], ALU.add))
                        dep(v.bn_stats(scal[:, 40:46], t1[:, 0:P]))
                        hold(v, "dve")
                        dep(v.bn_aggr(scal[:, 46:48], scal[:, 40:46]))
                        v.tensor_scalar(scal[:, 49:50], scal[:, 47:48], EPS, None, ALU.add).then_inc(sem("variance"), 1)
                        v.wait_ge(sem("deviation"), k + 1)
                        dep(v.reciprocal(scal[:, 51:52], scal[:, 50:51]))
                        if par == 0:
                            v.wait_ge(sem("out0"), 16 * pair) if not isinstance(pair, int) or pair else None
                        v.tensor_scalar(xo[:, par, 0:P], t1[:, 0:P], scal[:, 46:47], scal[:, 51:52], ALU.subtract, ALU.mult)\
                            .then_inc(sem("block_done"), 1)
                    assert did[0] == DEPS[s], did
                blocks(v, finish_block)





def kernel(**inputs):
    import concourse.bacc as bacc
    from concourse.bass_utils import run_bass_kernel_spmd

    nc = bacc.Bacc("TRN2", target_bir_lowering=False, num_devices=1)
    arrays = {}

    def put(name):
        a = np.ascontiguousarray(inputs[name])
        arrays["in_" + name] = a
        return nc.dram_tensor("in_" + name, a.shape, mybir.dt.from_np(a.dtype), kind="ExternalInput").ap()

    x, src, dst = put("x"), put("src"), put("dst")
    params = []
    for n in (1, 2, 3):
        names = {"W": f"W{n}", "as": f"as{n}", "ad": f"ad{n}", "b": f"b{n}", "sW": f"s{n}W", "sb": f"s{n}b"}
        params.append({k: put("L0_gnn_" + v) for k, v in names.items()})
    out = nc.dram_tensor("out_0", (N, D_OUT), F32, kind="ExternalOutput").ap()
    build(nc, x, src, dst, params, out)
    r = run_bass_kernel_spmd(nc, [arrays], core_ids=[0])
    return r.results[0]["out_0"]
```

```python
from contextlib import ExitStack

import numpy as np
import concourse.bass as bass
from concourse import mybir

F32 = mybir.dt.float32
I32 = mybir.dt.int32
ALU = mybir.AluOpType
ACT = mybir.ActivationFunctionType
AX = mybir.AxisListType

P = 128
N = 3125
NB = -(-N // P)
NP = NB * P
E = 53125
TILES = 416
TG = 104
NG4 = TILES // TG
W = 32
GT = P // W
BN = W - 1
CUTS = 544
CG = 68
NG8 = CUTS // CG
BIG = 1.0e30
SLOPE = 0.2
EPS = 1e-5
D_OUT = 128


class Layer:

    def __init__(self, number, D, H, C, CT, tiles, before):
        self.number, self.D, self.H, self.C, self.CT, self.tiles = number, D, H, C, CT, tiles
        self.ND = D // P
        self.HC = H * C
        self.OUT = self.HC if number < 2 else C
        self.ROW = D + H
        self.CHUNKS = tiles // CT
        self.GROUPS = CT // GT
        self.HT = H * CT
        self.MASKS = H + 2
        self.tile0 = tiles * number
        self.group0 = self.tile0 // GT
        self.chunk0 = sum(b.CHUNKS for b in before)
        self.slot0 = 16 * self.tile0 // 2
        self.mask0 = 16 * sum(b.MASKS * b.CHUNKS // 2 for b in before)
        self.QW = self.ND * H * W
        self.Q = self.ND * H


def three_layers(tiles):
    layers = []
    for number, (D, H, C, CT) in enumerate(((128, 4, 64, 16), (256, 4, 64, 16), (256, 6, 128, 8))):
        layers.append(Layer(number, D, H, C, CT, tiles, list(layers)))
    return layers


LAYERS = three_layers(TILES)
LAYERS_CUT = three_layers(CUTS)


def wide(ap, axis, shape):
    return ap.unsqueeze(axis).broadcast_to(shape)


def build(nc, x, src, dst, params, out):
    ctx = ExitStack()
    with ctx:
        sems = {}

        def sem(name):
            if name not in sems:
                sems[name] = ctx.enter_context(nc.semaphore(name))
            return sems[name]

        def sb(name, shape, dt=F32):
            return ctx.enter_context(nc.sbuf_tensor(name, shape, dt))

        table = [nc.dram_tensor(f"table{l.number}", (NP, l.ROW), F32, kind="Internal").ap() for l in LAYERS]
        dtable = [nc.dram_tensor(f"dtable{l.number}", (NP, l.H), F32, kind="Internal").ap() for l in LAYERS]
        xT_d = [nc.dram_tensor(f"xT{l.number}_d", (l.D, NP), F32, kind="Internal").ap() for l in LAYERS]
        masks_d = nc.dram_tensor("masks_d", (CUTS, 257), F32, kind="Internal").ap()
        rows_d = nc.dram_tensor("rows_d", (TILES, 3 * P), F32, kind="Internal").ap()
        joins_d = nc.dram_tensor("joins_d", (2, CUTS), F32, kind="Internal").ap()

        acc = sb("acc", [P, 12 * NP])
        dm = sb("dm", [6, NP])
        ring = sb("ring", [P, 4224])
        edges = sb("edges", [P, 3 * CUTS])
        idx = edges[:, 0:CUTS].bitcast(I32)
        dloc = edges[:, CUTS:2 * CUTS]
        factE = edges[:, 2 * CUTS:3 * CUTS]
        islot = sb("islot", [P, 2, 16], I32)
        baseI = sb("baseI", [1, 2 + CUTS], I32)
        ident = sb("ident", [P, P])
        iota = sb("iota", [P, W])
        spare = sb("spare", [1, 50], I32)
        ones = sb("ones", [1, P])
        vw = sb("vw", [P, 5 * 12])
        ARENA = 4744
        arena = sb("arena", [P, ARENA])
        used = [0]

        def carve(shape, dt=F32):
            size = int(np.prod(shape[1:]))
            a = arena[0:shape[0], used[0]:used[0] + size]
            used[0] += size
            assert used[0] <= ARENA, used[0]
            if len(shape) == 3:
                a = a.rearrange("p (a b) -> p a b", b=shape[2])
            return a

        one_t = carve([P, 2, P])
        sums_operands = carve([P, 2048])
        bblk = carve([P, 2, 64])
        mask = carve([96, 2, 257])
        joins = carve([1, 2, 16])
        sc = carve([P, 96])
        scl = sc
        mseg = carve([96, P])
        mrun = carve([96, P])
        fsc = mrun
        wT = carve([96, P])
        expo = wT
        wE = carve([P, 2, 96])
        fac = carve([P, 2, 96])
        fdg = carve([6, 96])
        facT = carve([6, 2, 16])
        firstcol = carve([6, 2])
        tmp = carve([P, 2, 12])
        qrow = carve([1, 4 * 17])
        arow = carve([1, 2, 4 * 17])
        urow = carve([1, 4 * 17])
        vrow = carve([1, 96])
        rrow = carve([1, 96])
        xrow = frow = vrow
        used[0] = 0
        t1 = carve([P, 768])
        xT = carve([P, 2, 256])
        xo = carve([P, 2, 262])
        bo = carve([P, 2, 6])
        xoT = carve([P, 2, 256])
        tsum = carve([P, 2, 256])
        all_scores = tsum.rearrange("p a b -> p (a b)")[:, 0:NB * 8].rearrange("p (b c) -> p b c", c=8)
        texp = carve([P, 2, 256])
        rden = carve([P, NB * 6])
        x0 = carve([P, 2, P])
        red = carve([P, P])
        stats = carve([P, 6])
        moment = carve([P, 2])
        moments = carve([P, NB, 2])
        scal = carve([P, NB])
        bias = carve([P, 512])

        ps = [ctx.enter_context(nc.psum_tensor(f"ps{i}", [P, 512], F32)) for i in range(8)]

        def g_rows(l):
            t = acc[:, 8 * NP:8 * NP + 2 * l.CT * l.ROW] if l.number == 1 else ring[:, 0:2 * l.CT * l.ROW]
            return t.rearrange("p (s c) -> p s c", c=l.ROW)

        def weighted_of(l, g):
            return sums_operands[:, g % 2 * GT * l.H * W:(g % 2 + 1) * GT * l.H * W]

        def onehots_of(l, par):
            at = 2 * GT * l.H * W + par * l.CT * W
            return sums_operands[:, at:at + l.CT * W]

        def sums(l):
            return acc[:, 0:l.Q * NP].rearrange("p (q n) -> p q n", n=NP)

        wts = ring[:, 0:1792]

        def ab(l, par):
            if l.number == 2 and par == 1:
                return edges[:, 0:1536]
            at = 1792 + par * l.Q * P
            return ring[:, at:at + l.Q * P]

        def prep(k, width=512, dt=F32):
            a = ring[0:TG, k * 512:k * 512 + NG4 * (width // 4)]
            if dt is I32:
                a = a.bitcast(I32)
            return a.rearrange("p (g e) -> p g e", g=NG4)

        srcR, dstR = prep(0, dt=I32), prep(1, dt=I32)
        srcF, dstF, lastR = prep(2), prep(3), prep(4)
        mt = prep(5, width=4 * 257)
        factR = arena[0:TG, 4180:4692].rearrange("p (g e) -> p g e", g=NG4)
        nextI, nextF = arena[0:TG, 4700:4704].bitcast(I32), arena[0:TG, 4704:4708]
        rows4 = acc[0:1, 8 * NP:8 * NP + 4 * TILES].rearrange("p (k t) -> p k t", t=TILES)
        dstE = ring[:, 3600:3600 + TILES]
        iotaI = ring[:, 4032:4032 + W].bitcast(I32)
        tail = 12 * NP - 5632
        wofs, aofs, o = [], [], tail
        for l in LAYERS:
            wofs.append(o)
            o += l.ND * l.HC
        for l in LAYERS:
            aofs.append(o)
            o += 2 * l.HC
        prod = acc[:, o:o + 768]
        assert o + 768 <= 12 * NP

        def vvec(l):
            o = (0, 12, 36)[l.number]
            return vw[:, o:o + l.ND * 2 * l.H].rearrange("p (d h) -> p d h", h=2 * l.H)

        used[0] = 8 * NP

        def cut_carve(shape, dt=F32):
            size = int(np.prod(shape[1:]))
            a = acc[0:shape[0], used[0]:used[0] + size]
            used[0] += size
            assert used[0] <= 12 * NP, used[0]
            if dt is I32:
                a = a.bitcast(I32)
            if len(shape) == 3:
                a = a.rearrange("p (a b) -> p a b", b=shape[2])
            return a

        cutR = cut_carve([CG, NG8, 3 * P])
        cutS, cutD, cutF = cutR[:, :, 0:P], cutR[:, :, P:2 * P], cutR[:, :, 2 * P:3 * P]
        cutN = cut_carve([CG, NG8, P])
        cutL = cut_carve([CG, NG8, P])
        cutX = cut_carve([CG, NG8, P])
        cutM = cut_carve([CG, NG8, 257])
        cutE = cut_carve([P, CUTS])
        cut4 = cut_carve([1, 4, CUTS])
        cutB = cut_carve([P, TILES])
        cutT = cut_carve([P, TILES])
        bound = cut_carve([P, 1])
        boundI = cut_carve([P, 1], I32)
        listI = cut_carve([P, TILES], I32)
        numI = cut_carve([CG, NG8], I32)
        num = cut_carve([CG, NG8])
        fromT = cut_carve([CG, NG8])
        fromI = cut_carve([CG, NG8], I32)
        low = cut_carve([CG, NG8])
        high = cut_carve([CG, NG8])
        firstF = cut_carve([1, TILES])
        squares = cut_carve([P, P])

        block = ctx.enter_context(nc.Block())

        CREDIT = {"turned": 8, "turned_used": 8, "turned_copied": 8, "expo_ready": 2, "summed": 32,
                  "window": 16, "merged": 8, "row_out0": 16, "row_out1": 16, "scores_out": 2, "heads_done": 2,
                  "skip_done": 2, "row_scored": 2, "row_turned": 2, "row_copied": 2, "scaled": 2, "preact": 2, "elu": 2,
                  "features": 2, "rows0": 16, "rows1": 16, "xT_out0": 16, "xT_out1": 16, "scores_kept": 2}

        def after(name, count):
            return CREDIT.get(name, 0) + count

        def give(eng, *names):
            for name in names:
                eng.sem_inc(sem(name), CREDIT[name])

        def give_dma(eng, at, *names):
            for k, name in enumerate(names):
                eng.dma_start(spare[0:1, at + 8 * k:at + 8 * k + 8],
                              src[0:8].unsqueeze(0)).then_inc(sem(name), CREDIT[name])

        def hold(eng, name):
            eng.sem_inc(sem("held_" + name), 1)

        def chunks(eng, l, chunk):
            half = l.CHUNKS // 2
            chunk(0, 0, 0, True)
            chunk(1, 0, 1, True)
            with eng.Fori(1, half - 1) as i:
                chunk(2 * i, i, 0, True)
                chunk(2 * i + 1, i, 1, True)
            chunk(l.CHUNKS - 2, half - 1, 0, True)
            chunk(l.CHUNKS - 1, half - 1, 1, False)

        def first_chunk(c):
            return isinstance(c, int) and c == 0

        def following(c, pair, par):
            return c + 1, pair + par, 1 - par

        def pipeline(eng, *stages):
            lags = [lag for lag, _ in stages]
            first, end = -(-max(lags) // 2), (NB + min(lags)) // 2

            def peeled(i):
                for lag, stage in stages:
                    if 0 <= i - lag < NB:
                        stage(i - lag, (i - lag) // 2, (i - lag) % 2)
            for i in range(min(lags), 2 * first):
                peeled(i)
            with eng.Fori(first, end) as j:
                for u in range(2):
                    for lag, stage in stages:
                        par = (u - lag) % 2
                        pair = j + (u - lag - par) // 2
                        stage(2 * j + (u - lag), pair, par)
            for i in range(2 * end, NB + max(lags)):
                peeled(i)

        STEP_SLOTS = {
            16: {"pe": (0, 2, 4, 5, 7, 9, 11), "dve": (0, 1, 5, 6, 8, 10, 12), "act": (1, 3, 9, 10)},
            8: {"pe": (0, 1, 3, 4, 5, 6), "dve": (0, 3, 4, 5, 6, 7), "act": (1, 5, 6)},
        }
        ACT_LAG, DVE_LAG = 1, 2

        def due(engine, CT, t):
            return [k for k, at in enumerate(STEP_SLOTS[CT][engine]) if at == t]

        def bases(eng, l, c, lag=0):
            _, values = nc.values_load_multi_w_load_instructions(
                baseI[0:1, bass.ds(c * l.CT + DVE_LAG - lag, l.CT)], engines=[eng.engine], min_val=0, max_val=N,
                skip_runtime_bounds_check_because="destinations are node numbers")
            return values

        PAIRS = (NB - NB // 2, NB // 2)
        def pairs_before(l, c, g):
            return l.group0 // 2 + c * (l.GROUPS // 2) + g // 2

        def table0_stored(eng):
            eng.wait_ge(sem("features_out"), 32)
            eng.wait_ge(sem("scores_stored"), 32)
            for par in range(2):
                eng.wait_ge(sem(f"xT_out{par}"), after(f"xT_out{par}", 16 * PAIRS[par]))

        def agg_done(eng, l):
            eng.wait_ge(sem("window"), after("window", 4 * (l.tile0 + l.tiles)))
            eng.wait_ge(sem("merged"), after("merged", l.tile0 + l.tiles))

        def either(eng, layers, cut):
            eng.wait_ge(sem("cut_known"), 1)
            _, (cut_needed,) = nc.values_load_multi_w_load_instructions(
                spare[0:1, 32:33], engines=[eng.engine], min_val=0, max_val=1,
                skip_runtime_bounds_check_because="the flag is 0 or 1")
            with eng.If(cut_needed > 0):
                cut(eng)
                layers(LAYERS_CUT)
            with eng.Else():
                layers(LAYERS)


        def cut_sp(sp):
            sp.wait_ge(sem("cut_masks"), 1)
            sp.dma_start(masks_d.rearrange("(g p) c -> p g c", p=CG), cutM).then_inc(sem("cut_out"), 16)
            sp.wait_ge(sem("cut_dst"), 2)
            sp.dma_start(cut4[:, 0, :], cutE[P - 1:P, :]).then_inc(sem("cut_lasts"), 16)
            sp.wait_ge(sem("cut_joins"), 1)
            sp.dma_start(joins_d.unsqueeze(0), cut4[:, 2:4, :]).then_inc(sem("cut_out"), 16)
            sp.wait_ge(sem("cut_out"), 32)
            sp.wait_ge(sem("cut_ready"), 1)

        def cut_pool(pool):
            pool.wait_ge(sem("vectors"), 10)
            pool.iota(boundI, pattern=[[0, 1]], base=BN, channel_multiplier=BN).then_inc(sem("cut_iota"), 1)
            pool.iota(listI, pattern=[[1, TILES]], base=0, channel_multiplier=0).then_inc(sem("cut_iota"), 1)
            pool.iota(numI, pattern=[[CG, NG8]], base=0, channel_multiplier=1).then_inc(sem("cut_iota"), 1)
            pool.wait_ge(sem("cut_from"), 1)
            hold(pool, "pool")
            for g in range(NG8):
                pool.indirect_dma_start(out=cutR[:, g, :], out_offset=None, in_=rows_d,
                                        in_offset=bass.IndirectOffsetOnAxis(ap=fromI[:, g:g + 1], axis=0)
                                        ).then_inc(sem("cut_rows"), 16)
            pool.wait_ge(sem("cut_ready"), 1)

        def cut_act(act):
            act.wait_ge(sem("cut_ready"), 1)

        def cut_pe(pe):
            pe.wait_ge(sem("cut_first"), 1)
            nc.tensor.matmul(ps[0][:, 0:TILES], lhsT=ones[0:1, :], rhs=firstF, start=True, stop=True).then_inc(sem("cut_spread"), 1)
            pe.wait_ge(sem("cut_begun"), 1)
            nc.tensor.matmul(ps[1][:, 0:TILES], lhsT=squares, rhs=cutB, start=True, stop=True).then_inc(sem("cut_counted"), 1)
            half = CG * (NG8 - 1)
            for k, (name, rows) in enumerate((("cut_edges", cutD), ("cut_edges", cutS), ("cut_factor", cutF))):
                pe.wait_ge(sem(name), 1)
                for g in range(NG8):
                    at = ps[2 + k][:, g * CG:(g + 1) * CG] if g < NG8 - 1 else ps[5 + k][:, 0:CG]
                    nc.tensor.transpose(at, rows[:, g, :], ident[0:CG, 0:CG]).then_inc(sem("cut_turned"), 1)
            pe.wait_ge(sem("cut_dst"), 2)
            nc.tensor.matmul(ps[0][:, 0:half], lhsT=ones[0:1, :], rhs=cutE[0:1, 0:half], start=True, stop=True).then_inc(sem("cut_firsts"), 1)
            nc.tensor.matmul(ps[1][:, 0:CG], lhsT=ones[0:1, :], rhs=cutE[0:1, half:CUTS], start=True, stop=True).then_inc(sem("cut_firsts"), 1)
            pe.wait_ge(sem("cut_ready"), 1)

        def cut_v(v):
            step = [0]

            def link(ins):
                step[0] += 1
                ins.then_inc(sem("cut_step"), 1)
                v.wait_ge(sem("cut_step"), step[0])

            v.tensor_copy(firstF, baseI[:, DVE_LAG:DVE_LAG + TILES]).then_inc(sem("cut_first"), 1)
            v.wait_ge(sem("cut_iota"), 3)
            link(v.memset(squares, 1.0))
            link(v.tensor_copy(bound, boundI))
            link(v.tensor_copy(num, numI))
            link(v.tensor_copy(cutT, listI))
            v.wait_ge(sem("cut_spread"), 1)
            v.tensor_scalar(cutB, ps[0][:, 0:TILES], bound, None, ALU.is_ge).then_inc(sem("cut_begun"), 1)
            v.wait_ge(sem("cut_counted"), 1)
            link(v.tensor_tensor(cutT, cutT, ps[1][:, 0:TILES], ALU.add))
            for g in range(NG8):
                link(v.tensor_scalar(cutB[0:CG, :], cutT[0:CG, :], num[:, g:g + 1], None, ALU.is_le))
                link(v.tensor_reduce(fromT[:, g:g + 1], cutB[0:CG, :], axis=AX.X, op=ALU.add))
            link(v.tensor_scalar(fromT, fromT, -1.0, None, ALU.add))
            v.tensor_copy(fromI, fromT).then_inc(sem("cut_from"), 1)
            link(v.tensor_tensor(high, num, fromT, ALU.subtract))
            link(v.tensor_scalar(low, high, float(BN), -1.0, ALU.mult, ALU.add))
            link(v.tensor_scalar(high, low, float(BN), None, ALU.add))
            link(v.tensor_scalar(low, low, float(N), None, ALU.min))
            lows, highs = wide(low, 2, [CG, NG8, P]), wide(high, 2, [CG, NG8, P])
            v.wait_ge(sem("cut_rows"), 16 * NG8)
            link(v.tensor_tensor(cutN, cutD, lows, ALU.is_le))
            link(v.tensor_tensor(cutX, cutD, highs, ALU.is_gt))
            link(v.tensor_tensor(cutN, cutN, cutX, ALU.add))
            link(v.tensor_tensor(cutD, cutD, lows, ALU.max))
            link(v.tensor_tensor(cutD, cutD, highs, ALU.min))
            link(v.tensor_tensor(cutX, cutD, cutS, ALU.subtract))
            link(v.tensor_tensor(cutX, cutX, cutN, ALU.mult))
            v.tensor_tensor(cutS, cutS, cutX, ALU.add).then_inc(sem("cut_edges"), 1)
            link(v.memset(cutL[:, :, P - 1:P], 1.0))
            link(v.tensor_tensor(cutL[:, :, 0:P - 1], cutD[:, :, 0:P - 1], cutD[:, :, 1:P], ALU.not_equal))
            link(v.memset(cutM[:, :, 0:1], -BIG))
            link(v.memset(cutM[:, :, P:P + 1], -BIG))
            link(v.tensor_scalar(cutM[:, :, 1:P], cutL[:, :, 0:P - 1], -BIG, None, ALU.mult))
            link(v.tensor_tensor(cutM[:, :, P + 1:2 * P + 1], cutD, cutD[:, :, 0:1].broadcast_to([CG, NG8, P]), ALU.not_equal))
            v.tensor_scalar(cutM[:, :, P + 1:2 * P + 1], cutM[:, :, P + 1:2 * P + 1], -BIG, None, ALU.mult).then_inc(sem("cut_masks"), 1)
            link(v.tensor_tensor(cutX, cutF, cutN, ALU.mult))
            v.tensor_tensor(cutF, cutF, cutX, ALU.subtract).then_inc(sem("cut_factor"), 1)
            v.wait_ge(sem("cut_turned"), 3 * NG8)
            half = CG * (NG8 - 1)
            v.tensor_copy(cutE[:, 0:half], ps[2][:, 0:half]).then_inc(sem("cut_dst"), 1)
            v.tensor_copy(cutE[:, half:CUTS], ps[5][:, 0:CG]).then_inc(sem("cut_dst"), 1)
            link(v.tensor_copy(idx[:, 0:half], ps[3][:, 0:half]))
            link(v.tensor_copy(idx[:, half:CUTS], ps[6][:, 0:CG]))
            link(v.tensor_copy(factE[:, 0:half], ps[4][:, 0:half]))
            link(v.tensor_copy(factE[:, half:CUTS], ps[7][:, 0:CG]))
            v.wait_ge(sem("cut_firsts"), 2)
            link(v.tensor_tensor(dloc[:, 0:half], cutE[:, 0:half], ps[0][:, 0:half], ALU.subtract))
            link(v.tensor_tensor(dloc[:, half:CUTS], cutE[:, half:CUTS], ps[1][:, 0:CG], ALU.subtract))
            link(v.tensor_copy(baseI[:, DVE_LAG:DVE_LAG + CUTS], cutE[0:1, :]))
            v.wait_ge(sem("cut_lasts"), 16)
            link(v.memset(cut4[:, 2, 0:1], 1.0))
            link(v.tensor_tensor(cut4[:, 2, 1:CUTS], cutE[0:1, 1:CUTS], cut4[:, 0, 0:CUTS - 1], ALU.not_equal))
            link(v.tensor_tensor(cut4[:, 1, :], cutE[0:1, :], cut4[:, 0, :], ALU.not_equal))
            link(v.tensor_tensor(cut4[:, 3, :], cut4[:, 1, :], cut4[:, 2, :], ALU.add))
            v.tensor_scalar(cut4[:, 2:4, :], cut4[:, 2:4, :], -BIG, None, ALU.mult).then_inc(sem("cut_joins"), 1)
            v.wait_ge(sem("cut_joins"), 1)
            v.sem_inc(sem("cut_ready"), 1)

        @block.sync
        def _(sp):
            give_dma(sp, 0, "row_out0", "row_out1")
            give_dma(sp, 34, "xT_out0", "xT_out1")
            sp.wait_ge(sem("pad_set"), 2)
            for rows, arr in ((srcR, src), (dstR, dst)):
                whole = 3 * TG * P
                left = E - whole
                sp.dma_start(rows[:, 0:3, :], arr[0:whole].rearrange("(g p e) -> p g e", g=3, p=TG)).then_inc(sem("edges_in"), 16)
                sp.dma_start(rows[0:left // P, 3, :], arr[whole:whole + left // P * P].rearrange("(p e) -> p e", e=P)).then_inc(sem("edges_in"), 16)
                sp.dma_start(rows[left // P:left // P + 1, 3, 0:left % P],
                             arr[whole + left // P * P:E].rearrange("(p e) -> p e", p=1)).then_inc(sem("edges_in"), 16)
            sp.wait_ge(sem("nexts_clear"), 1)
            sp.dma_start(nextI[:, 0:3].unsqueeze(2), dst[P:P + 3 * TG * P].rearrange("(g p e) -> p g e", g=3, p=TG)[:, :, 0:1], allow_slow_non_contiguous=True).then_inc(sem("nexts_in"), 16)
            sp.dma_start(nextI[0:TG - 2, 3:4], dst[P * (3 * TG + 1):P * (TILES - 1)].rearrange("(p e) -> p e", e=P)[:, 0:1], allow_slow_non_contiguous=True).then_inc(sem("nexts_in"), 16)
            sp.dma_start(nextI[TG - 2:TG - 1, 3:4], dst[P * (TILES - 1):P * (TILES - 1) + 1].unsqueeze(0), allow_slow_non_contiguous=True).then_inc(sem("nexts_in"), 16)
            for l, o, a in zip(LAYERS, wofs, aofs):
                p = params[l.number]
                sp.dma_start(acc[:, o:o + l.ND * l.HC].rearrange("p (d c) -> p d c", c=l.HC),
                             p["W"].rearrange("(d p) c -> p d c", p=P)).then_inc(sem("weights_in" if l.number else "weights_in0"), 16)
                for k, name in enumerate(("as", "ad")):
                    row = p[name].rearrange("h c -> (h c)").unsqueeze(0).broadcast_to([P, l.HC])
                    sp.dma_start(acc[:, a + k * l.HC:a + (k + 1) * l.HC], row).then_inc(sem("weights_in" if l.number else "weights_in0"), 16)
            sp.wait_ge(sem("src_float"), 1)
            sp.wait_ge(sem("dst_float"), 1)
            sp.wait_ge(sem("factors_made"), 1)
            for k, rows in enumerate((srcF, dstF, factR)):
                sp.dma_start(rows_d[:, k * P:(k + 1) * P].rearrange("(g p) e -> p g e", p=TG), rows).then_inc(sem("edges_out"), 16)
            sp.wait_ge(sem("masks_made"), 3)
            sp.dma_start(masks_d[0:TILES, :].rearrange("(g p) c -> p g c", p=TG), mt).then_inc(sem("masks_out"), 16)
            sp.wait_ge(sem("joins_made"), 1)
            sp.dma_start(joins_d[:, 0:TILES].unsqueeze(0), rows4[:, 2:4, :]).then_inc(sem("masks_out"), 16)

            def load_tile_scores(l, c, pair, par):
                first = bases(sp, l, c)
                g1 = l.group0 + c * l.GROUPS
                n1 = l.chunk0 + c + 1
                sp.wait_ge(sem("turned_used"), after("turned_used", g1 - l.GROUPS))
                hold(sp, "sp")
                sp.wait_ge(sem("expo_ready"), after("expo_ready", n1 - 2))
                hold(sp, "sp")
                for t in range(l.CT):
                    j = t % GT
                    sp.dma_start(bblk[j * W:(j + 1) * W, par, t * l.H:(t + 1) * l.H],
                                 dtable[l.number][bass.ds(first[t], W), :]).then_inc(sem(f"bwin{par}"), 16)
                for h in range(l.H):
                    sp.dma_start(mask[h * l.CT:(h + 1) * l.CT, par, :],
                                 masks_d[bass.ds(c * l.CT, l.CT), :]).then_inc(sem(f"mask{par}"), 16)
                sp.dma_start(joins[0:1, par, 0:l.CT], joins_d[0:1, bass.ds(c * l.CT, l.CT)]).then_inc(sem(f"mask{par}"), 16)
                sp.dma_start(arow[0:1, par, 0:l.H * (l.CT + 1)].rearrange("p (h t) -> p h t", h=l.H)[:, :, 1:l.CT + 1],
                             wide(joins_d[1:2, bass.ds(c * l.CT, l.CT)], 1, [1, l.H, l.CT])).then_inc(sem(f"mask{par}"), 16)

            def load_block(l, k, pair, par):
                sp.wait_ge(sem("skip_done"), after("skip_done", NB * l.number + k + 1 - 2))
                hold(sp, "sp")
                sp.dma_start(xT[:, par, 0:l.D].rearrange("p (d n) -> p d n", n=P),
                             xT_d[l.number].rearrange("(d p) n -> p d n", p=P)[:, :, bass.ds(k * P, P)]).then_inc(sem(f"block_in{par}"), 16)

            def load_residual(k, pair, par):
                sp.wait_ge(sem("features"), after("features", NB * 2 + k + 1 - 2))
                hold(sp, "sp")
                sp.dma_start(x0[:, par, :], table[0][bass.ds(k * P, P), 0:P]).then_inc(sem(f"residual_in{par}"), 16)

            def store_rows(s, k, pair, par):
                l = LAYERS[s]
                sp.wait_ge(sem("scores_out"), after("scores_out", 2 * (NB * (s - 1) + k + 1)))
                hold(sp, "sp")
                sp.dma_start(table[s][bass.ds(k * P, P), :], xo[:, par, 0:l.ROW]).then_inc(sem(f"row_out{par}"), 16)
                sp.dma_start(dtable[s][bass.ds(k * P, P), :], bo[:, par, 0:l.H]).then_inc(sem(f"row_out{par}"), 16)
                sp.dma_start(xT_d[s].rearrange("(d p) n -> p d n", p=P)[:, :, bass.ds(k * P, P)],
                             xoT[:, par, 0:l.D].rearrange("p (d n) -> p d n", n=P)).then_inc(sem(f"row_out{par}"), 16)

            def store_transposed(k, pair, par):
                sp.wait_ge(sem("row_copied"), after("row_copied", k + 1))
                hold(sp, "sp")
                sp.dma_start(xT_d[0][:, bass.ds(k * P, P)], xoT[:, par, 0:P]).then_inc(sem(f"xT_out{par}"), 16)

            def load_input(k, pair, par):
                last = isinstance(k, int) and k == NB - 1
                rows = N - (NB - 1) * P if last else P
                sp.wait_ge(sem("row_turned"), after("row_turned", k + 1 - 2))
                if last:
                    sp.wait_ge(sem("last_rows_zero"), 1)
                hold(sp, "sp")
                sp.dma_start(xo[0:rows, par, 0:P], x[bass.ds(k * P, rows), :]).then_inc(sem(f"input{par}"), 16)

            sp.dma_start(table[0][0:N, 0:P], x).then_inc(sem("features_out"), 16)
            sp.wait_ge(sem("pad_rows_zero"), 1)
            sp.dma_start(table[0][N:NP, 0:P], t1[0:NP - N, 0:P]).then_inc(sem("features_out"), 16)
            pipeline(sp, (-2, load_input), (0, store_transposed))
            sp.wait_ge(sem("scores_kept"), after("scores_kept", NB))
            H0 = LAYERS[0].H
            sp.dma_start(table[0][:, P:P + H0].rearrange("(b p) h -> p b h", p=P), all_scores[:, :, 0:H0]).then_inc(sem("scores_stored"), 16)
            sp.dma_start(dtable[0].rearrange("(b p) h -> p b h", p=P), all_scores[:, :, H0:2 * H0]).then_inc(sem("scores_stored"), 16)

            def layers(plan):
                for l in plan:
                    s = l.number
                    sp.wait_ge(sem("masks_out"), 32)
                    sp.wait_ge(sem("layer_clear"), 2 * (s + 1))
                    if s == 0:
                        table0_stored(sp)
                    for par in range(2):
                        sp.wait_ge(sem(f"row_out{par}"), after(f"row_out{par}", 48 * PAIRS[par] * s))
                    sp.wait_ge(sem("bases_made"), 1)
                    load_tile_scores(l, 0, 0, 0)

                    def chunk(c, pair, par, more):
                        if more:
                            load_tile_scores(l, *following(c, pair, par))
                    chunks(sp, l, chunk)

                    agg_done(sp, l)
                    p = params[s]
                    sp.dma_start(wts[:, 0:l.ND * l.HC].rearrange("p (d c) -> p d c", c=l.HC),
                                 p["W"].rearrange("(d p) c -> p d c", p=P)).then_inc(sem("wts_in"), 16)
                    sp.dma_start(wts[:, l.ND * l.HC:l.ND * (l.HC + l.OUT)].rearrange("p (d c) -> p d c", c=l.OUT),
                                 p["sW"].rearrange("(d p) c -> p d c", p=P)).then_inc(sem("wts_in"), 16)
                    for k, name in enumerate(("b", "sb")):
                        sp.dma_start(bias[:, k * l.OUT:(k + 1) * l.OUT],
                                     p[name].unsqueeze(0).broadcast_to([P, l.OUT])).then_inc(sem("wts_in"), 16)
                    load = lambda k, pair, par: load_block(l, k, pair, par)
                    if s < 2:
                        pipeline(sp, (-1, load), (2, lambda k, pair, par: store_rows(s + 1, k, pair, par)))
                    else:
                        pipeline(sp, (-1, load), (0, load_residual))
                        for half, (b0, b1) in enumerate(((0, NB // 2), (NB // 2, NB - 1))):
                            sp.wait_ge(sem("normalized"), half + 1)
                            sp.dma_start(out[b0 * P:b1 * P, :].rearrange("(b p) c -> p b c", p=P),
                                         sums(l)[:, 0, b0 * P:b1 * P].rearrange("p (b c) -> p b c", c=P)).then_inc(sem("out"), 16)
                        sp.wait_ge(sem("normalized"), 3)
                        sp.dma_start(out[(NB - 1) * P:N, :], sums(l)[0:N - (NB - 1) * P, 0, (NB - 1) * P:NB * P]).then_inc(sem("out"), 16)

            either(sp, layers, cut_sp)
            sp.wait_ge(sem("out"), 48)

        @block.gpsimd
        def _(pool):
            give_dma(pool, 16, "rows0", "rows1")
            pool.memset(ident[:, :], 0.0).then_inc(sem("ident_zero"), 1)
            pool.wait_ge(sem("ident_zero"), 1)
            pool.affine_select(out=ident[:, :], in_=ident[:, :], compare_op=ALU.not_equal, fill=1.0, base=0,
                               pattern=[[-1, P]], channel_multiplier=1).then_inc(sem("ident"), 1)
            pool.iota(iotaI, pattern=[[1, W]], base=0, channel_multiplier=0).then_inc(sem("iota"), 1)
            pool.memset(acc[:, 0:4 * NP], 0.0).then_inc(sem("sums_zero"), 1)
            pool.memset(dm[:, :], 0.0).then_inc(sem("sums_zero"), 1)
            pool.memset(acc[:, 4 * NP:8 * NP], 0.0).then_inc(sem("sums_zero"), 1)
            pool.wait_ge(sem("row_turned"), after("row_turned", NB - 2))
            pool.memset(xo[:, 0, 0:P], 0.0).then_inc(sem("last_rows_zero"), 1)
            pool.wait_ge(sem("idx_made"), 1)
            pool.wait_ge(sem("edges_out"), 48)
            pool.wait_ge(sem("joins_made"), 1)
            pool.wait_ge(sem("masks_out"), 32)

            def layers(plan):
                for l in plan:
                    s = l.number
                    rows = g_rows(l)
                    for par in range(2):
                        pool.wait_ge(sem(f"row_out{par}"), after(f"row_out{par}", 48 * PAIRS[par] * s))
                    if s == 0:
                        table0_stored(pool)
                    hold(pool, "pool")

                    def gather(c, pair, par, more):
                        n = l.chunk0 + c
                        T = l.tile0 + c * l.CT
                        pool.wait_ge(sem(f"rows{par}"), after(f"rows{par}", l.slot0 + 16 * l.CT * pair))
                        hold(pool, "pool")
                        pool.tensor_copy(islot[:, par, 0:l.CT], idx[:, bass.ds(c * l.CT, l.CT)]).then_inc(sem("islot"), 1)
                        pool.wait_ge(sem("islot"), n + 1)
                        for t in range(l.CT):
                            pool.wait_ge(sem("summed"), after("summed", T - 2 * l.CT + t + 1))
                            hold(pool, "pool")
                            pool.indirect_dma_start(
                                out=rows[:, par * l.CT + t, :], out_offset=None, in_=table[s],
                                in_offset=bass.IndirectOffsetOnAxis(ap=islot[:, par, t:t + 1], axis=0)
                            ).then_inc(sem(f"rows{par}"), 16)
                    chunks(pool, l, gather)

            either(pool, layers, cut_pool)

        @block.scalar
        def _(act):
            give(act, "turned_copied", "window", "row_copied", "elu", "scores_kept")

            def rows_turned(s, k, pair, par):
                l = LAYERS[s]
                tb = NB * s + k
                act.wait_ge(sem("row_turned"), after("row_turned", tb + 1))
                act.wait_ge(sem("row_scored"), after("row_scored", tb + 1 - 2))
                if s == 0:
                    act.wait_ge(sem(f"xT_out{par}"), after(f"xT_out{par}", 16 * pair))
                else:
                    act.wait_ge(sem(f"row_out{par}"), after(f"row_out{par}", 48 * (PAIRS[par] * (s - 1) + pair)))
                hold(act, "act")
                nc.scalar.activation(xoT[:, par, 0:l.D], ps[4 + par][:, 0:l.D], ACT.Copy).then_inc(sem("row_copied"), 1)

            def keep_scores(k, pair, par):
                act.wait_ge(sem("row_scored"), after("row_scored", k + 1))
                hold(act, "act")
                nc.scalar.activation(all_scores[:, bass.ds(k, 1), :].rearrange("p b c -> p (b c)"), ps[6 + par][:, 0:8],
                                     ACT.Copy).then_inc(sem("scores_kept"), 1)

            pipeline(act, (0, lambda k, pair, par: rows_turned(0, k, pair, par)), (1, keep_scores))

            def layers(plan):
                for l in plan:
                    s = l.number
                    HT = l.HT
                    act.wait_ge(sem("bases_made"), 1)

                    def score_step(step, c, pair, par):
                        n = l.chunk0 + c
                        halves = l.GROUPS // 2
                        if step < halves:
                            gg = l.group0 + c * l.GROUPS + 2 * step
                            act.wait_ge(sem("turned"), after("turned", gg + 2))
                            act.wait_ge(sem("turned_used"), after("turned_used", gg))
                            nc.scalar.activation(one_t, ps[4][:, 0:2 * P].rearrange("p (g e) -> p g e", e=P),
                                                 ACT.Copy).then_inc(sem("turned_copied"), 1)
                        elif step == halves:
                            act.wait_ge(sem("chain_gap"), n + 1)
                            nc.scalar.activation(frow[:, 0:HT], xrow[:, 0:HT], ACT.Exp).then_inc(sem("factor"), 1)
                        else:
                            act.wait_ge(sem("expo_ready"), after("expo_ready", n + 1))
                            nc.scalar.activation(wT[0:HT, :], expo[0:HT, :], ACT.Exp).then_inc(sem("wT"), 1)

                    steps = l.GROUPS // 2 + 2
                    for k in range(steps):
                        score_step(k, 0, 0, 0)

                    def window(T, t, at, par, n_chunk):
                        z = ps[t % 4]
                        act.wait_ge(sem("summed"), after("summed", T + 1))
                        if t == 0:
                            act.wait_ge(sem("head_factor"), n_chunk + 1)
                        act.wait_ge(sem("window"), after("window", 4 * T))
                        nc.scalar.activation(firstcol[0:l.H, t % 2:t % 2 + 1], z[0:l.H, 416:417], ACT.Copy).then_inc(sem("window"), 1)
                        hold(act, "act")
                        nc.scalar.activation(sums(l)[:, :, bass.ds(at + 1, W - 1)],
                                             z[:, 0:l.QW].rearrange("p (q w) -> p q w", w=W)[:, :, 1:W],
                                             ACT.Copy).then_inc(sem("window"), 1)
                        nc.scalar.activation(dm[0:l.H, bass.ds(at + 1, W - 1)], z[0:l.H, 417:417 + W - 1],
                                             ACT.Copy).then_inc(sem("window"), 1)
                        act.wait_ge(sem("window"), after("window", 4 * T + 1))
                        hold(act, "act")
                        nc.scalar.activation(dm[0:l.H, bass.ds(at, 1)], dm[0:l.H, bass.ds(at, 1)], ACT.Identity,
                                             bias=firstcol[0:l.H, t % 2:t % 2 + 1], scale=facT[0:l.H, par, t:t + 1]).then_inc(sem("window"), 1)

                    def chunk(c, pair, par, more):
                        first = bases(act, l, c, ACT_LAG)
                        for t in range(l.CT):
                            if not (first_chunk(c) and t < ACT_LAG):
                                before = t < ACT_LAG
                                window(l.tile0 + c * l.CT + t - ACT_LAG, (t - ACT_LAG) % l.CT, first[t],
                                       1 - par if before else par, l.chunk0 + c - before)
                            if more:
                                for k in due("act", l.CT, t):
                                    score_step(k, *following(c, pair, par))
                        if not more:
                            last = bases(act, l, l.CHUNKS - 1)
                            window(l.tile0 + l.tiles - 1, l.CT - 1, last[-1], 1, l.chunk0 + l.CHUNKS - 1)
                    chunks(act, l, chunk)

                    agg_done(act, l)
                    hold(act, "act")

                    def copy_block(k, pair, par):
                        act.wait_ge(sem("heads_done"), after("heads_done", NB * s + k + 1 - 2))
                        hold(act, "act")
                        nc.scalar.activation(ab(l, par)[:, 0:l.Q * P].rearrange("p (q n) -> p q n", n=P),
                                             sums(l)[:, :, bass.ds(k * P, P)], ACT.Copy).then_inc(sem("sums_copied"), 1)

                    def exponentials(k, pair, par):
                        act.wait_ge(sem("preact"), after("preact", NB * s + k + 1))
                        act.wait_ge(sem("features"), after("features", NB * s + k + 1 - 2))
                        hold(act, "act")
                        nc.scalar.activation(texp[:, par, 0:l.OUT], tsum[:, par, 0:l.OUT], ACT.Exp).then_inc(sem("elu"), 1)

                    if s < 2:
                        pipeline(act, (-1, copy_block), (1, exponentials), (2, lambda k, pair, par: rows_turned(s + 1, k, pair, par)))
                    else:
                        pipeline(act, (-1, copy_block), (1, exponentials))
                        act.wait_ge(sem("variances"), 1)
                        nc.scalar.activation(scal, scal, ACT.Sqrt).then_inc(sem("deviations"), 1)

            either(act, layers, cut_act)

        @block.tensor
        def _(pe):
            give(pe, "turned", "turned_used", "summed", "heads_done", "skip_done", "row_scored", "row_turned")
            pe.wait_ge(sem("ident"), 1)
            for k, (name, rows) in enumerate((("dst_float", dstF), ("src_float", srcF), ("factors_made", factR))):
                pe.wait_ge(sem(name), 1)
                for g in range(NG4):
                    nc.tensor.transpose(ps[k][:, g * TG:(g + 1) * TG], rows[:, g, :], ident[0:TG, 0:TG]).then_inc(sem("edges_turned"), 1)
            pe.wait_ge(sem("ones"), 1)
            pe.wait_ge(sem("dstE"), 1)
            nc.tensor.matmul(ps[3][:, 0:TILES], lhsT=ones[0:1, :], rhs=dstE[0:1, :], start=True, stop=True).then_inc(sem("firsts"), 1)
            nc.tensor.matmul(ps[6][0:1, 0:TILES], lhsT=ident[:, P - 1:P], rhs=dstE, start=True, stop=True).then_inc(sem("firsts"), 1)
            pe.wait_ge(sem("vectors"), 2)

            def turn_rows(s, k, pair, par):
                l = LAYERS[s]
                if s == 0:
                    pe.wait_ge(sem(f"input{par}"), 16 * (pair + 1))
                else:
                    pe.wait_ge(sem("features"), after("features", NB * (s - 1) + k + 1))
                pe.wait_ge(sem("row_copied"), after("row_copied", NB * s + k + 1 - 2))
                hold(pe, "pe")
                for d in range(l.ND):
                    last = nc.tensor.transpose(ps[4 + par][:, d * P:(d + 1) * P], xo[:, par, d * P:(d + 1) * P], ident[:, :])
                last.then_inc(sem("row_turned"), 1)

            def score_rows(s, k, pair, par):
                l = LAYERS[s]
                tb = NB * s + k
                pe.wait_ge(sem("row_copied"), after("row_copied", tb + 1))
                if s == 0:
                    pe.wait_ge(sem("scores_kept"), after("scores_kept", k + 1 - 2))
                else:
                    pe.wait_ge(sem("scores_out"), after("scores_out", 2 * (tb - NB + 1 - 2)))
                for d in range(l.ND):
                    last = nc.tensor.matmul(ps[6 + par][:, 0:2 * l.H], lhsT=xoT[:, par, d * P:(d + 1) * P], rhs=vvec(l)[:, d, :],
                                            start=d == 0, stop=d == l.ND - 1)
                last.then_inc(sem("row_scored"), 1)

            pipeline(pe, (0, lambda k, pair, par: turn_rows(0, k, pair, par)), (1, lambda k, pair, par: score_rows(0, k, pair, par)))

            def layers(plan):
                for l in plan:
                    s, H, CT, HT = l.number, l.H, l.CT, l.HT
                    rows = g_rows(l)

                    def turn(c, par, g):
                        pe.wait_ge(sem("turned_copied"), after("turned_copied", pairs_before(l, c, g)))
                        pe.wait_ge(sem("onehots"), pairs_before(l, c, g) + 1)
                        for k in range(2):
                            nc.tensor.transpose(ps[4][:, k * P:k * P + P], onehots_of(l, par)[:, (g + k) * P:(g + k + 1) * P],
                                                ident[:, :]).then_inc(sem("turned"), 1)

                    def expand(c, pair, par, g):
                        gg = l.group0 + c * l.GROUPS + g
                        if g % 2 == 0:
                            pe.wait_ge(sem("turned_copied"), after("turned_copied", pairs_before(l, c, g) + 1))
                        if g == 0:
                            pe.wait_ge(sem(f"bwin{par}"), l.slot0 + 16 * CT * (pair + 1))
                        nc.tensor.matmul(ps[5][:, g * GT * H:(g + 1) * GT * H], lhsT=one_t[:, g % 2, :],
                                         rhs=bblk[:, par, g * GT * H:(g + 1) * GT * H], start=True, stop=True).then_inc(sem("turned_used"), 1)

                    half = l.GROUPS // 2
                    steps = half + 5

                    def score_step(step, c, pair, par):
                        n = l.chunk0 + c
                        if step <= half:
                            if step:
                                expand(c, pair, par, 2 * step - 2)
                                expand(c, pair, par, 2 * step - 1)
                            if step < half:
                                turn(c, par, 2 * step)
                        elif step == half + 1:
                            pe.wait_ge(sem("scored"), n + 1)
                            hold(pe, "pe")
                            nc.tensor.transpose(ps[6][0:HT, 0:P], scl[:, 0:HT], ident[:, :]).then_inc(sem("score_turned"), 1)
                        elif step == half + 2:
                            pe.wait_ge(sem("segmax"), n + 1)
                            hold(pe, "pe")
                            nc.tensor.transpose(ps[7][0:1, 0:HT], mseg[0:HT, 0:1], ident[0:HT, 0:HT]).then_inc(sem("ends"), 1)
                            nc.tensor.transpose(ps[7][0:1, 128:128 + HT], mseg[0:HT, P - 1:P], ident[0:HT, 0:HT]).then_inc(sem("ends"), 1)
                        elif step == half + 3:
                            pe.wait_ge(sem("running"), n + 1)
                            nc.tensor.matmul(ps[7][0:HT, 256:257], lhsT=rrow[:, 0:HT], rhs=ones[0:1, 0:1], start=True, stop=True).then_inc(sem("spread"), 1)
                            pe.wait_ge(sem("factor"), n + 1)
                            nc.tensor.matmul(ps[7][:, 384:384 + HT], lhsT=ones[0:1, :], rhs=frow[:, 0:HT], start=True, stop=True).then_inc(sem("spread"), 1)
                        else:
                            pe.wait_ge(sem("wT"), n + 1)
                            hold(pe, "pe")
                            nc.tensor.transpose(ps[6][:, 128:128 + HT], wT[0:HT, :], ident[0:HT, 0:HT]).then_inc(sem("weights_turned"), 1)

                    for k in range(steps):
                        score_step(k, 0, 0, 0)

                    def chunk(c, pair, par, more):
                        for t in range(CT):
                            T = l.tile0 + c * CT + t
                            g = t // GT
                            z = ps[t % 4]
                            pe.wait_ge(sem("weighted"), T + 1)
                            if t == 0:
                                pe.wait_ge(sem("weights"), l.chunk0 + c + 1)
                            pe.wait_ge(sem("window"), after("window", 4 * (T - 3)))
                            pe.wait_ge(sem("merged"), after("merged", T - 3))
                            w = weighted_of(l, g)[:, t % GT * H * W:(t % GT + 1) * H * W]
                            for d in range(l.ND):
                                nc.tensor.matmul(z[:, d * H * W:(d + 1) * H * W], lhsT=rows[:, par * CT + t, d * P:(d + 1) * P],
                                                 rhs=w, start=True, stop=True)
                            nc.tensor.matmul(z[0:H, 416:416 + W], lhsT=wE[:, par, t * H:(t + 1) * H],
                                             rhs=onehots_of(l, par)[:, t * W:(t + 1) * W], start=True, stop=True).then_inc(sem("summed"), 1)
                            if more:
                                for k in due("pe", CT, t):
                                    score_step(k, *following(c, pair, par))
                    chunks(pe, l, chunk)

                    agg_done(pe, l)
                    pe.wait_ge(sem("wts_in"), 64 * (s + 1))
                    Wv = wts[:, 0:l.ND * l.HC].rearrange("p (d c) -> p d c", c=l.HC)
                    sWv = wts[:, l.ND * l.HC:l.ND * (l.HC + l.OUT)].rearrange("p (d c) -> p d c", c=l.OUT)

                    pe.wait_ge(sem("vectors"), 10)
                    pe.wait_ge(sem("pads"), 2 * (s + 1))
                    for k in range(NB):
                        last = nc.tensor.transpose(ps[7][:, k * H:(k + 1) * H], dm[0:H, k * P:(k + 1) * P], ident[0:H, 0:H])
                    last.then_inc(sem("dm_turned"), 1)
                    pe.wait_ge(sem("rden"), 2 * (s + 1))
                    halves = ((0, 0, 3), (2, 3, 6)) if s == 2 else ((0, 0, 4),)

                    def head_products(k, pair, par):
                        eb = NB * s + k
                        pe.wait_ge(sem("sums_copied"), eb + 1)
                        pe.wait_ge(sem("scaled"), after("scaled", eb + 1 - 2))
                        for bank, h0, h1 in halves:
                            for h in range(h0, h1):
                                at = (h - h0) * l.C
                                for d in range(l.ND):
                                    last = nc.tensor.matmul(ps[bank + par][:, at:at + l.C],
                                                            lhsT=ab(l, par)[:, (d * H + h) * P:(d * H + h + 1) * P],
                                                            rhs=Wv[:, d, h * l.C:(h + 1) * l.C], start=d == 0, stop=d == l.ND - 1)
                        last.then_inc(sem("heads_done"), 1)

                    def skip_product(k, pair, par):
                        pe.wait_ge(sem(f"block_in{par}"), 16 * (PAIRS[par] * s + pair + 1))
                        bank = ps[4 + par] if s == 2 else ps[2 + par]
                        for d in range(l.ND):
                            last = nc.tensor.matmul(bank[:, 0:l.OUT], lhsT=xT[:, par, d * P:(d + 1) * P], rhs=sWv[:, d, :],
                                                    start=d == 0, stop=d == l.ND - 1)
                        last.then_inc(sem("skip_done"), 1)

                    if s < 2:
                        pipeline(pe, (0, head_products), (2, lambda k, pair, par: turn_rows(s + 1, k, pair, par)),
                                 (0, skip_product), (2, lambda k, pair, par: score_rows(s + 1, k, pair, par)))
                    else:
                        pipeline(pe, (0, head_products), (0, skip_product))

            either(pe, layers, cut_pe)

        @block.vector
        def _(v):
            step = [0]

            def link(ins):
                step[0] += 1
                ins.then_inc(sem("prep_step"), 1)
                v.wait_ge(sem("prep_step"), step[0])

            give(v, "expo_ready", "merged", "scores_out", "scaled", "preact", "features")
            v.memset(t1[0:NP - N, 0:P], 0.0).then_inc(sem("pad_rows_zero"), 1)
            def score_vectors(layers):
                for l in layers:
                    o, a = wofs[l.number], aofs[l.number]
                    for k in range(2):
                        for d in range(l.ND):
                            v.tensor_tensor(prod[:, 0:l.HC], acc[:, o + d * l.HC:o + (d + 1) * l.HC],
                                            acc[:, a + k * l.HC:a + (k + 1) * l.HC], ALU.mult).then_inc(sem("vproduct"), 1)
                            v.wait_ge(sem("vproduct"), (0, 2, 6)[l.number] + k * l.ND + d + 1)
                            v.tensor_reduce(vvec(l)[:, d, k * l.H:(k + 1) * l.H], prod[:, 0:l.HC].rearrange("p (h c) -> p h c", c=l.C),
                                            axis=AX.X, op=ALU.add).then_inc(sem("vectors"), 1)
                            v.wait_ge(sem("vectors"), (0, 2, 6)[l.number] + k * l.ND + d + 1)

            v.memset(srcR[:, 3, :], 0).then_inc(sem("pad_set"), 1)
            v.memset(dstR[:, 3, :], N).then_inc(sem("pad_set"), 1)
            v.memset(ones[:, :], 1.0).then_inc(sem("ones"), 1)
            link(v.memset(nextI, -1))
            v.sem_inc(sem("nexts_clear"), 1)
            v.wait_ge(sem("edges_in"), 96)
            v.wait_ge(sem("nexts_in"), 48)
            link(v.tensor_copy(nextF, nextI))
            v.tensor_copy(dstF, dstR).then_inc(sem("dst_float"), 1)
            v.tensor_copy(srcF, srcR).then_inc(sem("src_float"), 1)
            v.wait_ge(sem("dst_float"), 1)
            link(v.tensor_tensor(lastR[:, :, P - 1:P], dstF[:, :, P - 1:P], nextF.unsqueeze(2), ALU.not_equal))
            v.tensor_tensor(lastR[:, :, 0:P - 1], dstF[:, :, 0:P - 1], dstF[:, :, 1:P], ALU.not_equal).then_inc(sem("last_made"), 1)
            v.wait_ge(sem("src_float"), 1)
            v.wait_ge(sem("last_made"), 1)
            link(v.tensor_tensor(factR, srcF, dstF, ALU.is_equal))
            link(v.tensor_tensor(factR, factR, lastR, ALU.mult))
            v.tensor_scalar(factR, factR, 1.0, None, ALU.add).then_inc(sem("factors_made"), 1)
            v.memset(mt[:, :, 0:1], -BIG).then_inc(sem("masks_made"), 1)
            v.memset(mt[:, :, P:P + 1], -BIG).then_inc(sem("masks_made"), 1)
            link(v.tensor_tensor(mt[:, :, P + 1:2 * P + 1], dstF, dstF[:, :, 0:1].broadcast_to([TG, NG4, P]), ALU.not_equal))
            link(v.tensor_scalar(mt[:, :, P + 1:2 * P + 1], mt[:, :, P + 1:2 * P + 1], -BIG, None, ALU.mult))
            v.wait_ge(sem("last_made"), 1)
            v.tensor_scalar(mt[:, :, 1:P], lastR[:, :, 0:P - 1], -BIG, None, ALU.mult).then_inc(sem("masks_made"), 1)
            v.wait_ge(sem("iota"), 1)
            link(v.tensor_copy(iota[:, :], iotaI))
            v.wait_ge(sem("edges_turned"), 12)
            v.tensor_copy(dstE, ps[0][:, 0:TILES]).then_inc(sem("dstE"), 1)
            v.tensor_copy(idx[:, 0:TILES], ps[1][:, 0:TILES]).then_inc(sem("idx_made"), 1)
            link(v.tensor_copy(factE[:, 0:TILES], ps[2][:, 0:TILES]))
            v.wait_ge(sem("dstE"), 1)
            link(v.memset(baseI[:, 0:DVE_LAG], 0))
            v.tensor_copy(baseI[:, DVE_LAG:DVE_LAG + TILES], dstE[0:1, :]).then_inc(sem("bases_made"), 1)
            v.wait_ge(sem("firsts"), 2)
            link(v.tensor_tensor(dloc[:, 0:TILES], dstE, ps[3][:, 0:TILES], ALU.subtract))
            v.wait_ge(sem("weights_in0"), 48)
            score_vectors(LAYERS[0:1])
            link(v.tensor_copy(rows4[:, 0, :], ps[6][0:1, 0:TILES]))
            link(v.tensor_tensor(rows4[:, 2, :], rows4[:, 0, :], dstE[0:1, :], ALU.subtract))
            link(v.tensor_reduce(rows4[:, 3, 0:1], rows4[:, 2, :], axis=AX.X, op=ALU.max))
            v.tensor_scalar(spare[0:1, 32:33], rows4[:, 3, 0:1], float(W), None, ALU.is_ge).then_inc(sem("cut_known"), 1)
            v.wait_ge(sem("cut_known"), 1)
            link(v.memset(rows4[:, 2, 0:1], 1.0))
            link(v.tensor_tensor(rows4[:, 2, 1:TILES], dstE[0:1, 1:TILES], rows4[:, 0, 0:TILES - 1], ALU.not_equal))
            link(v.tensor_tensor(rows4[:, 1, :], dstE[0:1, :], rows4[:, 0, :], ALU.not_equal))
            link(v.tensor_tensor(rows4[:, 3, :], rows4[:, 1, :], rows4[:, 2, :], ALU.add))
            v.tensor_scalar(rows4[:, 2:4, :], rows4[:, 2:4, :], -BIG, None, ALU.mult).then_inc(sem("joins_made"), 1)
            def scores_out(s, k, pair, par):
                l = LAYERS[s]
                tb = NB * s + k
                v.wait_ge(sem("row_scored"), after("row_scored", tb + 1))
                v.wait_ge(sem(f"row_out{par}"), after(f"row_out{par}", 48 * (PAIRS[par] * (s - 1) + pair)))
                v.tensor_copy(xo[:, par, l.D:l.ROW], ps[6 + par][:, 0:l.H]).then_inc(sem("scores_out"), 1)
                v.tensor_copy(bo[:, par, 0:l.H], ps[6 + par][:, l.H:2 * l.H]).then_inc(sem("scores_out"), 1)

            v.wait_ge(sem("weights_in"), 96)
            score_vectors(LAYERS[1:])
            table0_stored(v)
            v.memset(vrow[:, :], 0.0)
            v.memset(urow[:, :], 0.0).then_inc(sem("carry_clear"), 1)

            def layers(plan):
                for l in plan:
                    s, H, CT, HT, C1 = l.number, l.H, l.CT, l.HT, l.CT + 1
                    rows = g_rows(l)
                    half = l.GROUPS // 2
                    steps = half + 5
                    by_head = lambda a: a.rearrange("p (h t) -> p h t", h=H)
                    with_carry = lambda a: a[:, 0:H * C1].rearrange("p (h t) -> p h t", h=H)

                    for par in range(2):
                        v.wait_ge(sem(f"row_out{par}"), after(f"row_out{par}", 48 * PAIRS[par] * s))
                    v.memset(arow, -BIG).then_inc(sem("layer_clear"), 1)
                    v.memset(bblk[:, :, :], 0.0).then_inc(sem("layer_clear"), 1)
                    v.wait_ge(sem("layer_clear"), 2 * (s + 1))
                    v.wait_ge(sem("bases_made"), 1)

                    def onehots(c, par, g):
                        v.tensor_tensor(onehots_of(l, par)[:, g * P:(g + 2) * P].rearrange("p (t w) -> p t w", w=W),
                                        wide(iota[:, :], 1, [P, 2 * GT, W]),
                                        wide(dloc[:, bass.ds(c * CT + g * GT, 2 * GT)], 2, [P, 2 * GT, W]),
                                        ALU.is_equal).then_inc(sem("onehots"), 1)

                    def score_step(step, c, pair, par):
                        n = l.chunk0 + c
                        if step < half:
                            if step == 0:
                                v.wait_ge(sem("summed"), after("summed", l.tile0 + (c - 1) * CT))
                            onehots(c, par, 2 * step)
                        elif step == half:
                            v.wait_ge(sem("turned_used"), after("turned_used", l.group0 + (c + 1) * l.GROUPS))
                            v.wait_ge(sem(f"rows{par}"), after(f"rows{par}", l.slot0 + 16 * CT * (pair + 1)))
                            v.tensor_tensor(by_head(sc[:, 0:HT]), rows[:, par * CT:(par + 1) * CT, l.D:l.ROW].rearrange("p t h -> p h t"),
                                            ps[5][:, 0:HT].rearrange("p (t h) -> p h t", h=H), ALU.add).then_inc(sem("score_sum"), 1)
                            v.wait_ge(sem("score_sum"), n + 1)
                            v.scalar_tensor_tensor(out=scl[:, 0:HT], in0=sc[:, 0:HT], scalar=SLOPE, in1=sc[:, 0:HT],
                                                   op0=ALU.mult, op1=ALU.max).then_inc(sem("scored"), 1)
                        elif step == half + 1:
                            v.wait_ge(sem("score_turned"), n + 1)
                            v.wait_ge(sem(f"mask{par}"), l.mask0 + 16 * l.MASKS * (pair + 1))
                            v.tensor_tensor_scan(fsc[0:HT, :], mask[0:HT, par, 0:P], ps[6][0:HT, 0:P], 0.0,
                                                 ALU.add, ALU.max).then_inc(sem("forward"), 1)
                            v.wait_ge(sem("forward"), n + 1)
                            v.tensor_tensor_scan(mseg[0:HT, ::-1], mask[0:HT, par, P:0:-1], fsc[0:HT, ::-1], 0.0,
                                                 ALU.add, ALU.max).then_inc(sem("segmax"), 1)
                        elif step == half + 2:
                            v.tensor_copy(with_carry(qrow)[:, :, 0:1], with_carry(urow)[:, :, CT:C1]).then_inc(sem("chain_in"), 1)
                            v.wait_ge(sem("ends"), 2 * (n + 1))
                            v.tensor_copy(with_carry(qrow)[:, :, 1:C1], by_head(ps[7][0:1, 128:128 + HT])).then_inc(sem("chain_in"), 1)
                            v.wait_ge(sem("chain_in"), 2 * (n + 1))
                            v.tensor_tensor_scan(urow[:, 0:H * C1], arow[:, par, 0:H * C1], qrow[:, 0:H * C1], 0.0,
                                                 ALU.add, ALU.max).then_inc(sem("chain"), 1)
                            v.wait_ge(sem("chain"), n + 1)
                            v.tensor_tensor(by_head(vrow[:, 0:HT]), with_carry(urow)[:, :, 0:CT], wide(joins[:, par, 0:CT], 1, [1, H, CT]),
                                            ALU.add).then_inc(sem("incoming"), 1)
                            v.wait_ge(sem("incoming"), n + 1)
                            v.tensor_tensor(rrow[:, 0:HT], vrow[:, 0:HT], ps[7][0:1, 0:HT], ALU.max).then_inc(sem("running"), 1)
                            v.wait_ge(sem("running"), n + 1)
                            v.tensor_tensor(xrow[:, 0:HT], vrow[:, 0:HT], rrow[:, 0:HT], ALU.subtract).then_inc(sem("chain_gap"), 1)
                        elif step == half + 3:
                            v.wait_ge(sem("spread"), 2 * (n + 1))
                            v.scalar_tensor_tensor(out=mrun[0:HT, :], in0=mask[0:HT, par, P + 1:2 * P + 1], scalar=ps[7][0:HT, 256:257],
                                                   in1=mseg[0:HT, :], op0=ALU.add, op1=ALU.max).then_inc(sem("run_max"), 1)
                            v.tensor_copy(fac[:, par, 0:HT], ps[7][:, 384:384 + HT]).then_inc(sem("factors"), 1)
                            v.wait_ge(sem("run_max"), n + 1)
                            v.tensor_tensor(expo[0:HT, :], ps[6][0:HT, 0:P], mrun[0:HT, :], ALU.subtract).then_inc(sem("expo_ready"), 1)
                            v.wait_ge(sem("factors"), n + 1)
                            v.tensor_tensor(by_head(fdg[0:H, 0:HT]), by_head(fac[0:H, par, 0:HT]),
                                            wide(ident[0:H, 0:H], 2, [H, H, CT]), ALU.mult).then_inc(sem("own_factor"), 1)
                            v.wait_ge(sem("own_factor"), n + 1)
                            v.tensor_reduce(facT[0:H, par, 0:CT], fdg[0:H, 0:HT].rearrange("p (h t) -> p t h", h=H),
                                            axis=AX.X, op=ALU.add).then_inc(sem("head_factor"), 1)
                        else:
                            v.wait_ge(sem("weights_turned"), n + 1)
                            v.tensor_tensor(wE[:, par, 0:HT].rearrange("p (t h) -> p t h", h=H),
                                            ps[6][:, 128:128 + HT].rearrange("p (h t) -> p t h", h=H),
                                            wide(factE[:, bass.ds(c * CT, CT)], 2, [P, CT, H]), ALU.mult).then_inc(sem("weights"), 1)

                    def weight(c, pair, par, g):
                        gg = l.group0 + c * l.GROUPS + g
                        v.wait_ge(sem("summed"), after("summed", GT * (gg - 1)))
                        if g == 0:
                            v.wait_ge(sem("weights"), l.chunk0 + c + 1)
                            v.wait_ge(sem("onehots"), pairs_before(l, c, 0) + half)
                        for t in range(GT):
                            w = wE[:, par, (g * GT + t) * H:(g * GT + t + 1) * H]
                            last = v.tensor_tensor(weighted_of(l, g)[:, t * H * W:(t + 1) * H * W].rearrange("p (h w) -> p h w", w=W),
                                                   wide(onehots_of(l, par)[:, (g * GT + t) * W:(g * GT + t + 1) * W], 1, [P, H, W]),
                                                   wide(w, 2, [P, H, W]), ALU.mult)
                            last.then_inc(sem("weighted"), 1)

                    for k in range(steps):
                        score_step(k, 0, 0, 0)
                    weight(0, 0, 0, 0)

                    def merge(T, t, par, at):
                        z = ps[t % 4]
                        v.wait_ge(sem("window"), after("window", 4 * T + 4))
                        v.wait_ge(sem("merged"), after("merged", T))
                        v.tensor_tensor(tmp[:, t % 2, 0:l.Q].rearrange("p (d h) -> p d h", h=H),
                                        sums(l)[:, :, bass.ds(at, 1)].rearrange("p (d h) o -> p d (h o)", h=H),
                                        wide(fac[:, par, 0:HT].rearrange("p (h t) -> p t h", h=H)[:, t, :], 1, [P, l.ND, H]),
                                        ALU.mult).then_inc(sem("kept"), 1)
                        v.wait_ge(sem("kept"), T + 1)
                        v.tensor_tensor(sums(l)[:, :, bass.ds(at, 1)].rearrange("p q o -> p (q o)"), tmp[:, t % 2, 0:l.Q],
                                        z[:, 0:l.QW].rearrange("p (q w) -> p q w", w=W)[:, :, 0], ALU.add).then_inc(sem("merged"), 1)

                    def chunk(c, pair, par, more):
                        first = bases(v, l, c, DVE_LAG)
                        for t in range(CT):
                            if more:
                                for k in due("dve", CT, t):
                                    score_step(k, *following(c, pair, par))
                            if t % GT == 0 and t // GT + 1 < l.GROUPS:
                                weight(c, pair, par, t // GT + 1)
                            if t == DVE_LAG:
                                v.wait_ge(sem("head_factor"), l.chunk0 + c + 1)
                            if not (first_chunk(c) and t < DVE_LAG):
                                merge(l.tile0 + c * CT + t - DVE_LAG, (t - DVE_LAG) % CT, par if t >= DVE_LAG else 1 - par, first[t])
                        if more:
                            c2, pair2, par2 = following(c, pair, par)
                            weight(c2, pair2, par2, 0)
                        else:
                            last = bases(v, l, l.CHUNKS - 1)
                            for t in range(CT - DVE_LAG, CT):
                                merge(l.tile0 + l.tiles - CT + t, t, par, last[t])
                    chunks(v, l, chunk)

                    agg_done(v, l)
                    v.memset(sums(l)[:, :, N:NP], 0.0).then_inc(sem("pads"), 1)
                    v.memset(dm[:, N:NP], 0.0).then_inc(sem("pads"), 1)
                    v.wait_ge(sem("pads"), 2 * (s + 1))
                    v.wait_ge(sem("wts_in"), 64 * (s + 1))
                    v.tensor_tensor(bias[:, 0:l.OUT], bias[:, 0:l.OUT], bias[:, l.OUT:2 * l.OUT], ALU.add).then_inc(sem("bias_made"), 1)
                    v.wait_ge(sem("bias_made"), s + 1)
                    r = rden[:, 0:NB * H]
                    v.wait_ge(sem("dm_turned"), s + 1)
                    v.tensor_scalar(r, ps[7][:, 0:NB * H], 1e-16, None, ALU.add).then_inc(sem("rden"), 1)
                    v.wait_ge(sem("rden"), 2 * s + 1)
                    v.reciprocal(r, r).then_inc(sem("rden"), 1)
                    v.wait_ge(sem("rden"), 2 * s + 2)

                    def chain(name, per_block):
                        def start(k):
                            done = [0]

                            def dep(ins):
                                done[0] += 1
                                assert done[0] <= per_block
                                ins.then_inc(sem(f"{name}{s}"), 1)
                                v.wait_ge(sem(f"{name}{s}"), per_block * k + done[0])
                            return dep
                        return start

                    combining = chain("combine", 1 if s < 2 else 3)
                    activating = chain("activate", 1 if s < 2 else 5)

                    def combine(k, pair, par):
                        eb = NB * s + k
                        dep = combining(k)
                        v.wait_ge(sem("elu"), after("elu", eb + 1 - 2))
                        v.wait_ge(sem("heads_done"), after("heads_done", eb + 1))
                        hold(v, "dve")
                        t = tsum[:, par, 0:l.OUT]
                        if s < 2:
                            dep(v.tensor_tensor(t1[:, 0:l.HC].rearrange("p (h c) -> p h c", c=l.C),
                                                ps[par][:, 0:l.HC].rearrange("p (h c) -> p h c", c=l.C),
                                                wide(rden[:, bass.ds(k * H, H)], 2, [P, H, l.C]), ALU.mult))
                            v.wait_ge(sem("skip_done"), after("skip_done", eb + 1))
                            v.tensor_tensor(t, t1[:, 0:l.HC], ps[2 + par][:, 0:l.OUT], ALU.add).then_inc(sem("scaled"), 1)
                        else:
                            for half in range(2):
                                last = v.tensor_tensor(t1[:, half * 384:(half + 1) * 384].rearrange("p (h c) -> p h c", c=l.C),
                                                       ps[2 * half + par][:, 0:384].rearrange("p (h c) -> p h c", c=l.C),
                                                       wide(rden[:, bass.ds(k * H + 3 * half, 3)], 2, [P, 3, l.C]), ALU.mult)
                                dep(last)
                            dep(v.tensor_reduce(red[:, :], t1[:, 0:l.HC].rearrange("p (h c) -> p c h", c=l.C), axis=AX.X, op=ALU.add))
                            v.wait_ge(sem("skip_done"), after("skip_done", eb + 1))
                            v.scalar_tensor_tensor(out=t, in0=red[:, :], scalar=1.0 / H, in1=ps[4 + par][:, 0:l.OUT],
                                                   op0=ALU.mult, op1=ALU.add).then_inc(sem("scaled"), 1)
                        v.wait_ge(sem("scaled"), after("scaled", eb + 1))
                        v.tensor_tensor(t, t, bias[:, 0:l.OUT], ALU.add).then_inc(sem("preact"), 1)

                    def activate(k, pair, par):
                        eb = NB * s + k
                        dep = activating(k)
                        v.wait_ge(sem("elu"), after("elu", eb + 1))
                        e, t = texp[:, par, 0:l.OUT], tsum[:, par, 0:l.OUT]
                        dep(v.tensor_scalar(e, e, 1.0, -1.0, ALU.min, ALU.add))
                        if s < 2:
                            v.wait_ge(sem(f"row_out{par}"), after(f"row_out{par}", 48 * (PAIRS[par] * s + pair)))
                            v.tensor_tensor(xo[:, par, 0:l.OUT], t, e, ALU.max).then_inc(sem("features"), 1)
                        else:
                            y = sums(l)[:, 0, bass.ds(k * P, P)]
                            v.wait_ge(sem(f"residual_in{par}"), 16 * (pair + 1))
                            dep(v.tensor_tensor(e, t, e, ALU.max))
                            dep(v.tensor_tensor(red, e, x0[:, par, :], ALU.add))
                            v.tensor_copy(y, red).then_inc(sem("kept_sum"), 1)
                            dep(v.bn_stats(stats, red))
                            hold(v, "dve")
                            dep(v.bn_aggr(moment, stats))
                            hold(v, "dve")
                            v.tensor_copy(moments[:, bass.ds(k, 1), :].rearrange("p a b -> p (a b)"), moment).then_inc(sem("features"), 1)

                    if s < 2:
                        pipeline(v, (0, combine), (1, activate), (2, lambda k, pair, par: scores_out(s + 1, k, pair, par)))
                    else:
                        pipeline(v, (0, combine), (1, activate))
                        v.wait_ge(sem("features"), after("features", 3 * NB))
                        v.wait_ge(sem("kept_sum"), NB)
                        v.tensor_scalar(scal, moments[:, :, 1], EPS, None, ALU.add).then_inc(sem("variances"), 1)
                        v.wait_ge(sem("deviations"), 1)
                        v.reciprocal(scal, scal).then_inc(sem("inverse"), 1)
                        v.wait_ge(sem("inverse"), 1)
                        for k in range(NB):
                            y = sums(l)[:, 0, k * P:(k + 1) * P]
                            last = v.tensor_scalar(y, y, moments[:, k, 0:1], scal[:, k:k + 1], ALU.subtract, ALU.mult)
                            if k in (NB // 2 - 1, NB - 2, NB - 1):
                                last.then_inc(sem("normalized"), 1)

            either(v, layers, cut_v)

def kernel(**inputs):
    import concourse.bacc as bacc
    from concourse.bass_utils import run_bass_kernel_spmd

    nc = bacc.Bacc("TRN2", target_bir_lowering=False, num_devices=1)
    arrays = {}

    def put(name):
        a = np.ascontiguousarray(inputs[name])
        arrays["in_" + name] = a
        return nc.dram_tensor("in_" + name, a.shape, mybir.dt.from_np(a.dtype), kind="ExternalInput").ap()

    x, src, dst = put("x"), put("src"), put("dst")
    params = []
    for n in (1, 2, 3):
        names = {"W": f"W{n}", "as": f"as{n}", "ad": f"ad{n}", "b": f"b{n}", "sW": f"s{n}W", "sb": f"s{n}b"}
        params.append({k: put("L0_gnn_" + v) for k, v in names.items()})
    out = nc.dram_tensor("out_0", (N, D_OUT), F32, kind="ExternalOutput").ap()
    build(nc, x, src, dst, params, out)
    r = run_bass_kernel_spmd(nc, [arrays], core_ids=[0])
    return r.results[0]["out_0"]
```
